# Optimizing a Trainium2 kernel written in Bass

```python
import numpy as np
import jax
import jax.numpy as jnp

def _softmax(x, axis=-1):
    return jax.nn.softmax(x, axis=axis)

def _gelu(x):
    return jax.nn.gelu(x, approximate=True)

def _silu(x):
    return jax.nn.silu(x)

def _sigmoid(x):
    return jax.nn.sigmoid(x)

def _layernorm(x, axis=-1, eps=1e-05):
    m = jnp.mean(x, axis=axis, keepdims=True)
    v = jnp.var(x, axis=axis, keepdims=True)
    return (x - m) / jnp.sqrt(v + eps)

def _scatter_add(tgt, idx, src, axis=0):
    return tgt.at[idx].add(src)

def _segment_sum(src, seg, n):
    return jax.ops.segment_sum(src, seg, n)
kernel_name = 'mk_cond_seq_d1_seqx_r8_bbfb42'

def setup_inputs(seed: int=0):
    np.random.seed(seed)
    _w = jnp.asarray

    def _rec_inputs():
        import jax
        import jax.numpy as jnp
        _rk = jax.random.key(seed)
        x = 1.648e-05 + 1 * jax.random.normal(jax.random.fold_in(_rk, 1), (16, 128, 144), jnp.float32)
        _lenS = 128 - jax.random.randint(jax.random.fold_in(_rk, 7), (16,), 0, max(1, 128 // 4) + 1, jnp.int32)
        _lenS2 = 128 - jax.random.randint(jax.random.fold_in(_rk, 8), (16,), 0, max(1, 128 // 4) + 1, jnp.int32)
        cond_1152 = 0.00914911 + 1.00357 * jax.random.normal(jax.random.fold_in(_rk, 11), (16, 144), jnp.float32)
        return (x, cond_1152)
    x, cond_1152 = _rec_inputs()

    def _L0_cond_setup():
        import jax, jax.numpy as jnp
        import numpy as np
        B, N, D = (8, 128, 144)
        H = 16
        HD = D // H
        HID = 4 * D
        EPS = 1e-06

        def _ln(x):
            mu = jnp.mean(x, axis=-1, keepdims=True)
            var = jnp.mean(jnp.square(x - mu), axis=-1, keepdims=True)
            return (x - mu) * jax.lax.rsqrt(var + EPS)

        def _modulate(x, shift, scale):
            return x * (1.0 + scale[:, None, :]) + shift[:, None, :]

        def _attn(x, w_qkv, b_qkv, w_proj, b_proj):
            b, n, d = x.shape
            qkv = (x @ w_qkv + b_qkv).reshape(b, n, 3, H, HD)
            q = qkv[:, :, 0].transpose(0, 2, 1, 3)
            k = qkv[:, :, 1].transpose(0, 2, 1, 3)
            v = qkv[:, :, 2].transpose(0, 2, 1, 3)
            scores = jnp.einsum('bhnd,bhmd->bhnm', q, k) * HD ** (-0.5)
            attn = jax.nn.softmax(scores, axis=-1)
            out = jnp.einsum('bhnm,bhmd->bhnd', attn, v)
            out = out.transpose(0, 2, 1, 3).reshape(b, n, d)
            return out @ w_proj + b_proj
        key = jax.random.key(seed)
        ks = jax.random.split(key, 12)
        s = 0.02
        return {'x': jax.random.normal(ks[0], (B, N, D), jnp.float32), 't_emb': jax.random.normal(ks[1], (B, D), jnp.float32), 'w_qkv': jax.random.normal(ks[2], (D, 3 * D), jnp.float32) * s, 'b_qkv': jax.random.normal(ks[3], (3 * D,), jnp.float32) * s, 'w_proj': jax.random.normal(ks[4], (D, D), jnp.float32) * s, 'b_proj': jax.random.normal(ks[5], (D,), jnp.float32) * s, 'w_fc1': jax.random.normal(ks[6], (D, HID), jnp.float32) * s, 'b_fc1': jax.random.normal(ks[7], (HID,), jnp.float32) * s, 'w_fc2': jax.random.normal(ks[8], (HID, D), jnp.float32) * s, 'b_fc2': jax.random.normal(ks[9], (D,), jnp.float32) * s, 'w_ada': jax.random.normal(ks[10], (D, 6 * D), jnp.float32) * s, 'b_ada': jax.random.normal(ks[11], (6 * D,), jnp.float32) * s}
    _L0_cond_all = _L0_cond_setup()
    _L0_cond_in = {k: v for k, v in _L0_cond_all.items() if k in ('w_qkv', 'b_qkv', 'w_proj', 'b_proj', 'w_fc1', 'b_fc1', 'w_fc2', 'b_fc2', 'w_ada', 'b_ada')}
    del _L0_cond_all
    return {'x': x, 'cond_1152': cond_1152, 'L0_cond_w_qkv': _L0_cond_in['w_qkv'], 'L0_cond_b_qkv': _L0_cond_in['b_qkv'], 'L0_cond_w_proj': _L0_cond_in['w_proj'], 'L0_cond_b_proj': _L0_cond_in['b_proj'], 'L0_cond_w_fc1': _L0_cond_in['w_fc1'], 'L0_cond_b_fc1': _L0_cond_in['b_fc1'], 'L0_cond_w_fc2': _L0_cond_in['w_fc2'], 'L0_cond_b_fc2': _L0_cond_in['b_fc2'], 'L0_cond_w_ada': _L0_cond_in['w_ada'], 'L0_cond_b_ada': _L0_cond_in['b_ada']}

def reference(x, cond_1152, L0_cond_w_qkv, L0_cond_b_qkv, L0_cond_w_proj, L0_cond_b_proj, L0_cond_w_fc1, L0_cond_b_fc1, L0_cond_w_fc2, L0_cond_b_fc2, L0_cond_w_ada, L0_cond_b_ada):
    import jax
    import jax.numpy as jnp

    def _L0_cond_ref(x, t_emb, w_qkv, b_qkv, w_proj, b_proj, w_fc1, b_fc1, w_fc2, b_fc2, w_ada, b_ada):
        import jax, jax.numpy as jnp
        import numpy as np
        B, N, D = (8, 128, 144)
        H = 16
        HD = D // H
        HID = 4 * D
        EPS = 1e-06

        def _ln(x):
            mu = jnp.mean(x, axis=-1, keepdims=True)
            var = jnp.mean(jnp.square(x - mu), axis=-1, keepdims=True)
            return (x - mu) * jax.lax.rsqrt(var + EPS)

        def _modulate(x, shift, scale):
            return x * (1.0 + scale[:, None, :]) + shift[:, None, :]

        def _attn(x, w_qkv, b_qkv, w_proj, b_proj):
            b, n, d = x.shape
            qkv = (x @ w_qkv + b_qkv).reshape(b, n, 3, H, HD)
            q = qkv[:, :, 0].transpose(0, 2, 1, 3)
            k = qkv[:, :, 1].transpose(0, 2, 1, 3)
            v = qkv[:, :, 2].transpose(0, 2, 1, 3)
            scores = jnp.einsum('bhnd,bhmd->bhnm', q, k) * HD ** (-0.5)
            attn = jax.nn.softmax(scores, axis=-1)
            out = jnp.einsum('bhnm,bhmd->bhnd', attn, v)
            out = out.transpose(0, 2, 1, 3).reshape(b, n, d)
            return out @ w_proj + b_proj
        ada = jax.nn.silu(t_emb) @ w_ada + b_ada
        shift_a, scale_a, gate_a, shift_f, scale_f, gate_f = jnp.split(ada, 6, axis=-1)
        x = x + gate_a[:, None, :] * _attn(_modulate(_ln(x), shift_a, scale_a), w_qkv, b_qkv, w_proj, b_proj)
        h = _modulate(_ln(x), shift_f, scale_f)
        h = jax.nn.gelu(h @ w_fc1 + b_fc1, approximate=True) @ w_fc2 + b_fc2
        return x + gate_f[:, None, :] * h
    x = _L0_cond_ref(x, cond_1152, L0_cond_w_qkv, L0_cond_b_qkv, L0_cond_w_proj, L0_cond_b_proj, L0_cond_w_fc1, L0_cond_b_fc1, L0_cond_w_fc2, L0_cond_b_fc2, L0_cond_w_ada, L0_cond_b_ada)
    return x

_drawn_inputs = setup_inputs


def setup_inputs(seed=0):
    import zlib

    import numpy as np

    out = dict(_drawn_inputs(seed))
    spreads = {}
    factors = {'cond_1152': 6.282,
     'L0_cond_w_qkv': 8.0,
     'L0_cond_b_qkv': 8.0,
     'L0_cond_w_proj': 8.0,
     'L0_cond_b_proj': 64.0,
     'L0_cond_w_fc1': 6.696,
     'L0_cond_b_fc1': 62.879,
     'L0_cond_w_fc2': 6.605,
     'L0_cond_b_fc2': 64.0,
     'L0_cond_w_ada': 5.884,
     'L0_cond_b_ada': 8.0}
    for name, (base, spread) in spreads.items():
        noise = np.random.default_rng([zlib.crc32(name.encode()), seed]).standard_normal(out[name].shape)
        drawn = base * np.exp(spread * noise) if base else spread * noise
        out[name] = jnp.asarray(drawn.astype(out[name].dtype))
    for name, factor in factors.items():
        out[name] = (out[name] * factor).astype(out[name].dtype)
    return out
```

```python
from contextlib import ExitStack

import numpy as np

import concourse.bass as bass
from concourse import mybir

F32 = mybir.dt.float32
BF16 = mybir.dt.bfloat16
ACT = mybir.ActivationFunctionType
ALU = mybir.AluOpType
AX = mybir.AxisListType

B, N, D, H = 16, 128, 144, 16
HD = D // H
HID = 4 * D
P = 128
EPS = 1e-6
SCALE = float(HD) ** -0.5
LEFT = D - P
PARTS = 3
SPLIT_ROWS = 6 * LEFT
LROWS = SPLIT_ROWS + PARTS
GB = 2
GT = GB * N
GROUPS = B // GB
QKC = 3
QKR = 2 * D // QKC
PROD_ROWS = PARTS * PARTS * HD
MAX_ROW = 96
SROWS = MAX_ROW + PARTS
QUADS = H // 4
VW = HD + 1
SLOTS = 4
HCH = [(0, 128), (128, 128), (256, 128), (384, 96), (480, 96)]
NCH = len(HCH)
WCOLS = 3 * D + D + HID
C_V, C_P, C_F = 2 * D, 3 * D, 4 * D
BF16_ONES = float(np.array([0x3F803F80], np.uint32).view(np.float32)[0])
SPARE = 128


def build(nc, x, cond, w_all, w_fc2, w_ada, masks, out):
    ctx = ExitStack()
    with ctx:
        def sb(name, shape, dt=F32):
            return ctx.enter_context(nc.sbuf_tensor(name, shape, dt))

        def sem(name):
            return ctx.enter_context(nc.semaphore(name))

        bank = [ctx.enter_context(nc.psum_tensor(f"bank{i}", [P, 512], F32)) for i in range(8)]

        parts_d = nc.dram_tensor("parts_d", [B, PARTS + 2, HD, 2, H, N], BF16, kind="Internal").ap()
        left_d = nc.dram_tensor("left_d", [B, 4 * LEFT], F32, kind="Internal").ap()
        gate_d = nc.dram_tensor("gate_d", [B, 2 * D], F32, kind="Internal").ap()

        ident = sb("ident", [P, P])
        ident_b = sb("ident_b", [P, P], BF16)
        zeros = sb("zeros", [P, H])
        epsilon = sb("epsilon", [P, GB])
        mhalf = sb("mhalf", [P, B])
        msk = sb("msk", [LROWS, 2])
        wm = sb("wm", [P, WCOLS])
        wl = sb("wl", [LROWS, WCOLS], BF16)
        wlf = sb("wlf", [LROWS, WCOLS])
        wlr = sb("wlr", [LROWS, WCOLS])
        wlb = sb("wlb", [LROWS, WCOLS], BF16)
        w2 = sb("w2", [P, NCH, D])
        wa = sb("wa", [P, 6 * D])
        wal = sb("wal", [LEFT + 1, 6 * D])
        cs = sb("cs", [B, D])
        ce = sb("ce", [B, D])
        cr = sb("cr", [B, D])
        ct = sb("ct", [P, B])
        ctl = sb("ctl", [LEFT + 1, B])
        mod = sb("mod", [P, 4, B])
        left_r = sb("left_r", [B, 4 * LEFT])
        gate_r = sb("gate_r", [B, 2 * D])
        bl = sb("bl", [P, B, 4 * LEFT])
        gates = sb("gates", [P, B, 2 * D])
        xs = sb("xs", [P, B, D])
        x1 = sb("x1", [P, B, D])
        st = sb("st", [P, B, 6])
        mv = sb("mv", [P, B, 2])
        ve = sb("ve", [P, B])
        rs = sb("rs", [P, B])
        st2 = sb("st2", [P, 2, GB, 6])
        mv2 = sb("mv2", [P, 2, GB, 2])
        ve2 = sb("ve2", [P, 2, GB])
        rs2 = sb("rs2", [P, 2, GB])
        xn = sb("xn", [P, 2, GB, D])
        lm = sb("lm", [P, GB, LEFT])
        lv = sb("lv", [P, GB, LEFT])
        lr = sb("lr", [P, GB, LEFT])
        lt = sb("lt", [P, 2, GB, LROWS], BF16)
        ht = sb("ht", [P, 2, GT])
        hl = sb("hl", [LROWS, 2, GT], BF16)
        qkp = sb("qkp", [QKR, 2, PARTS, QKC, GT], BF16)
        qkr = sb("qkr", [QKR, 2, QKC, GT])
        v_all = sb("v_all", [P, B, H, VW])
        qt = sb("qt", [P, SLOTS, H * N], BF16)
        kt = sb("kt", [P, SLOTS, H * N], BF16)
        vt = sb("vt", [P, SLOTS, H, VW])
        xr = sb("xr", [P, SLOTS, D])
        nm = sb("nm", [P, 2, H])
        nmr = sb("nmr", [P, H])
        nmp = sb("nmp", [P, 2, PARTS, H], BF16)
        nmt = sb("nmt", [PARTS * H, N], BF16)
        ex = sb("ex", [P, QUADS, 4 * N])
        ot = sb("ot", [P, QUADS * N])
        rd = sb("rd", [P, H])
        at = sb("at", [P, D])
        alr = sb("alr", [P, LEFT])
        alt = sb("alt", [P, LROWS], BF16)
        att = sb("att", [P, N])
        atl = sb("atl", [LROWS, N], BF16)
        pr = sb("pr", [P, D])
        hg = sb("hg", [P, 2, NCH, GT])
        fr = sb("fr", [P, 2, GB, D])
        yo = sb("yo", [P, 2, GB, D])

        passed = sem("passed")
        cond_in, wa_in, wm_in, wrest_in, wl_in, w2_in, x_in = (sem(n) for n in (
            "cond_in", "wa_in", "wm_in", "wrest_in", "wl_in", "w2_in", "x_in"))
        consts, ident_zero, cleared, set_by_dve = sem("consts"), sem("ident_zero"), sem("cleared"), sem("set_by_dve")
        silu_exp, silu_step, silu_ready = sem("silu_exp"), sem("silu_step"), sem("silu_ready")
        ct_turned, ct_copied, ada_done, mod_ready = sem("ct_turned"), sem("ct_copied"), sem("ada_done"), sem("mod_ready")
        rows_ready, rows_out, bl_in, gates_in = sem("rows_ready"), sem("rows_out"), sem("bl_in"), sem("gates_in")
        wl_step, wl_ready = sem("wl_step"), sem("wl_ready")
        stat_step, mv_ready, ve_ready, rs_ready = sem("stat_step"), sem("mv_ready"), sem("ve_ready"), sem("rs_ready")
        xn_ready = [sem("xn_ready0"), sem("xn_ready2")]
        left_step = [sem("left_step0"), sem("left_step2")]
        left_ready = [sem("left_ready0"), sem("left_ready2")]
        xt_done = [sem("xt_done0"), sem("xt_done2")]
        ht_ready = [sem("ht_ready0"), sem("ht_ready2")]
        hl_ready = [sem("hl_ready0"), sem("hl_ready2")]
        qk_done, hi_ready, rest_ready, mid_ready, lo_ready = (sem(n) for n in (
            "qk_done", "hi_ready", "rest_ready", "mid_ready", "lo_ready"))
        v_done, v_copied, ones_set = sem("v_done"), sem("v_copied"), sem("ones_set")
        parts_out = [sem(f"parts_out{p}") for p in range(2)]
        qk_in, v_in, xr_in = ([sem(f"{n}{k}") for k in range(SLOTS)] for n in ("qk_in", "v_in", "xr_in"))
        max_in = sem("max_in")
        s_done, max_ready, nm_step, nm_ready = sem("s_done"), sem("max_ready"), sem("nm_step"), sem("nm_ready")
        nmt_done, nmt_copied = sem("nmt_done"), sem("nmt_copied")
        st_done, ex_ready, pv_done, ot_copied = sem("st_done"), sem("ex_ready"), sem("pv_done"), sem("ot_copied")
        on_done, rd_ready, at_ready = sem("on_done"), sem("rd_ready"), sem("at_ready")
        alt_step, alt_ready, att_done, att_copied = sem("alt_step"), sem("alt_ready"), sem("att_done"), sem("att_copied")
        proj_done, pr_ready, x1_ready = sem("proj_done"), sem("pr_ready"), sem("x1_ready")
        st2_done, mv2_ready, ve2_ready, rs2_ready = sem("st2_done"), sem("mv2_ready"), sem("ve2_ready"), sem("rs2_ready")
        f1_done, g_ready, f2_done, fr_ready, y_ready = (sem(n) for n in (
            "f1_done", "g_ready", "f2_done", "fr_ready", "y_ready"))
        y_out = [sem(f"y_out{p}") for p in range(2)]

        block = ctx.enter_context(nc.Block())

        x_tok = x.rearrange("b n d -> n b d")
        out_tok = out.rearrange("b n d -> n b d")

        def head(i, j):
            h = 4 * i + j
            return slice(h * N, (h + 1) * N)

        @block.sync
        def _(sp):
            for s in (*parts_out, *y_out):
                sp.sem_inc(s, SPARE)
            sp.dma_start(cs[:, :], cond).then_inc(cond_in, 16)
            sp.dma_start(wa[:, :], w_ada[0:P, :]).then_inc(wa_in, 16)
            sp.dma_start(wal[:, :], w_ada[P:D + 1, :]).then_inc(wa_in, 16)
            for q in range(4):
                sp.dma_start(xs[:, 4 * q:4 * q + 4, :], x_tok[:, 4 * q:4 * q + 4, :]).then_inc(x_in, 16)
            sp.dma_start(msk[:, :], masks).then_inc(wl_in, 16)
            lrows, brow = w_all[P:D, :], w_all[D:D + 1, :]
            sp.dma_start(wlf[0:SPLIT_ROWS, :], bass.AP(tensor=lrows.tensor, offset=lrows.offset,
                         ap=[[0, 6], [WCOLS, LEFT], [1, WCOLS]])).then_inc(wl_in, 16)
            sp.dma_start(wlf[SPLIT_ROWS:LROWS, :], bass.AP(tensor=brow.tensor, offset=brow.offset,
                         ap=[[0, PARTS], [1, WCOLS]])).then_inc(wl_in, 16)
            sp.dma_start(wm[:, 0:C_P], w_all[0:P, 0:C_P]).then_inc(wm_in, 16)
            sp.wait_ge(rows_ready, 6)
            sp.dma_start(left_d, left_r[:, :]).then_inc(rows_out, 16)
            sp.dma_start(gate_d, gate_r[:, :]).then_inc(rows_out, 16)
            sp.wait_ge(rows_out, 32)
            sp.dma_start(bl[:, :, :], bass.AP(tensor=left_d.tensor, offset=left_d.offset,
                         ap=[[0, P], [1, B * 4 * LEFT]])).then_inc(bl_in, 16)
            sp.dma_start(wm[:, C_P:WCOLS], w_all[0:P, C_P:WCOLS]).then_inc(wrest_in, 16)
            sp.dma_start(gates[:, :, :], bass.AP(tensor=gate_d.tensor, offset=gate_d.offset,
                         ap=[[0, P], [1, B * 2 * D]])).then_inc(gates_in, 16)
            sp.dma_start(w2[:, 0:3, :], w_fc2[0:3 * P, :].rearrange("(c p) n -> p c n", p=P)).then_inc(w2_in, 16)
            sp.dma_start(w2[0:96, 3, :], w_fc2[HCH[3][0]:HCH[4][0], :]).then_inc(w2_in, 16)
            sp.dma_start(w2[0:97, 4, :], w_fc2[HCH[4][0]:HID + 1, :]).then_inc(w2_in, 16)

            def parts_store(g, p):
                sp.wait_ge(lo_ready, QKC * (g + 1) + SPARE)
                for b in range(GB):
                    dst = parts_d[bass.ds(g * GB + b, 1)].rearrange("o l (c e) a h t -> (e a h) (o l c) t", c=QKC)
                    src = qkp[:, p, :, :, b * N:(b + 1) * N].rearrange("p l c t -> p (l c) t")
                    sp.dma_start(dst[:, 0:PARTS * QKC], src).then_inc(parts_out[p], 16)
                    sp.dma_start(dst[:, PARTS * QKC:(PARTS + 2) * QKC], src[:, 0:2 * QKC]).then_inc(parts_out[p], 16)

            with sp.Fori(0, GROUPS // 2) as i:
                for p in range(2):
                    parts_store(2 * i + p, p)

            def qk_load(b, slot):
                k = parts_d[bass.ds(b, 1), 0:PARTS, :, 1].rearrange("o l d h t -> (o l d) (h t)")
                q = parts_d[bass.ds(b, 1), 0:PARTS, :, 0].rearrange("o l d h t -> (o l d) (h t)")
                row, block_of = 2 * H * N, HD * 2 * H * N
                for tile, a, rot in ((kt, k, 0), (qt, q, block_of)):
                    src = bass.AP(tensor=a.tensor, offset=a.offset, ap=[[row, PARTS * HD], [rot, PARTS], [1, H * N]])
                    sp.dma_start(tile[0:PROD_ROWS, slot, :], src).then_inc(qk_in[slot], 16)

            def vx_load(b, slot):
                sp.dma_start(vt[:, slot], v_all[:, bass.ds(b, 1)].rearrange("p o h w -> p (o h) w")).then_inc(v_in[slot], 16)
                sp.dma_start(xr[:, slot], x_tok[:, bass.ds(b, 1), :].rearrange("p o d -> p (o d)")).then_inc(xr_in[slot], 16)

            def max_load(b, slot):
                sp.wait_ge(nmt_copied, b + 1)
                sp.dma_start(qt[MAX_ROW:SROWS, slot, :], nmt[:, :]).then_inc(max_in, 16)

            for p in range(2):
                sp.wait_ge(parts_out[p], SPARE + 64 * GROUPS // 2)
            sp.wait_ge(cleared, 2)
            for b in range(3):
                qk_load(b, b)
            sp.wait_ge(v_copied, SPARE + GROUPS)
            for b in range(2):
                vx_load(b, b)
            max_load(0, 0)

            def attention_loads(it, k, last):
                u = SLOTS * it + k
                if k + 1 < SLOTS or not last:
                    max_load(u + 1, (k + 1) % SLOTS)
                if k + 2 < SLOTS or not last:
                    sp.wait_ge(pv_done, 4 * (u - 1) + SPARE)
                    sp.sem_inc(passed, 1)
                    sp.wait_ge(x1_ready, u - 1 + SPARE)
                    sp.sem_inc(passed, 1)
                    vx_load(u + 2, (k + 2) % SLOTS)
                if k + 3 < SLOTS or not last:
                    sp.wait_ge(st_done, 4 * u + SPARE)
                    qk_load(u + 3, (k + 3) % SLOTS)

            with sp.Fori(0, B // SLOTS - 1) as i:
                for k in range(SLOTS):
                    attention_loads(i, k, False)
            for k in range(SLOTS):
                attention_loads(B // SLOTS - 1, k, True)

            with sp.Fori(0, GROUPS // 2) as i:
                for p in range(2):
                    g = 2 * i + p
                    sp.wait_ge(y_ready, GB * (g + 1) + SPARE)
                    sp.dma_start(out_tok[:, bass.ds(g * GB, GB), :], yo[:, p]).then_inc(y_out[p], 16)
            for p in range(2):
                sp.wait_ge(y_out[p], SPARE + 16 * GROUPS // 2)

        @block.gpsimd
        def _(pool):
            for s in (x1_ready, y_ready):
                pool.sem_inc(s, SPARE)
            nc.gpsimd.memset(ident[:, :], 0.0).then_inc(ident_zero, 1)
            nc.gpsimd.memset(ident_b[:, :], 0.0).then_inc(ident_zero, 1)
            pool.wait_ge(ident_zero, 2)
            for m in (ident, ident_b):
                nc.gpsimd.affine_select(out=m[:, :], in_=m[:, :], compare_op=ALU.not_equal, fill=1.0, base=0,
                                        pattern=[[-1, P]], channel_multiplier=1).then_inc(consts, 1)
            nc.gpsimd.memset(mhalf[:, :], -0.5).then_inc(ones_set, 1)
            nc.gpsimd.memset(zeros[:, :], 0.0).then_inc(ones_set, 1)
            nc.gpsimd.memset(epsilon[:, :], EPS).then_inc(ones_set, 1)
            nc.gpsimd.memset(lt[:, :, :, SPLIT_ROWS:LROWS], 1.0).then_inc(ones_set, 1)
            nc.gpsimd.memset(alt[:, SPLIT_ROWS:LROWS], 1.0).then_inc(ones_set, 1)
            nc.gpsimd.memset(v_all[:, :, :, HD:VW], 1.0).then_inc(ones_set, 1)
            pool.wait_ge(ones_set, 6)
            nc.gpsimd.memset(kt[64:MAX_ROW, :, :].bitcast(F32), 0.0).then_inc(cleared, 1)
            nc.gpsimd.memset(qt[64:MAX_ROW, :, :].bitcast(F32), 0.0).then_inc(cleared, 1)
            pool.wait_ge(cleared, 2)

            pool.wait_ge(mv_ready, B)
            nc.gpsimd.tensor_scalar(ve[:, :], mv[:, :, 1], EPS, None, ALU.add).then_inc(ve_ready, 1)
            pool.wait_ge(ve_ready, 1)
            pool.wait_ge(ones_set, 6)
            nc.gpsimd.tensor_tensor(rs[:, :], ve[:, :], mhalf[:, :], ALU.pow).then_inc(rs_ready, 1)

            def left_parts(ph, g, p):
                step = left_step[ph]
                shift, scale = 2 * ph * LEFT, (2 * ph + 1) * LEFT
                sh = bl[:, bass.ds(g * GB, GB), shift:shift + LEFT]
                L = lt[:, p, :, 0:SPLIT_ROWS].rearrange("p b (r w) -> p b r w", w=LEFT)
                a1 = L[:, :, 0]

                def times(v, r):
                    return v[:, :, None, :].to_broadcast([P, GB, r, LEFT])

                pool.wait_ge(xn_ready[ph], g + 1)
                nc.gpsimd.tensor_tensor(lm[:, :, :], xn[:, p, :, P:D], bl[:, bass.ds(g * GB, GB), scale:scale + LEFT],
                                        ALU.mult).then_inc(step, 1)
                pool.wait_ge(step, 4 * g + 1)
                nc.gpsimd.tensor_tensor(lv[:, :, :], lm[:, :, :], sh, ALU.add).then_inc(step, 1)
                nc.gpsimd.tensor_tensor(L[:, :, 0:3], times(lm, 3), times(sh, 3), ALU.add).then_inc(step, 1)
                pool.wait_ge(step, 4 * g + 3)
                nc.gpsimd.tensor_tensor(lr[:, :, :], lv[:, :, :], a1, ALU.subtract).then_inc(step, 1)
                nc.gpsimd.tensor_tensor(L[:, :, 3:5], times(lv, 2), times(a1, 2), ALU.subtract).then_inc(left_ready[ph], 1)
                pool.wait_ge(step, 4 * g + 4)
                pool.wait_ge(left_ready[ph], 2 * g + 1)
                nc.gpsimd.tensor_tensor(L[:, :, 5], lr[:, :, :], L[:, :, 3], ALU.subtract).then_inc(left_ready[ph], 1)

            pool.wait_ge(bl_in, 16)
            left_parts(0, 0, 0)
            left_parts(0, 1, 1)

            def pool_phase0(g, p):
                pool.wait_ge(xt_done[0], g + 1)
                left_parts(0, g + 2, p)

            with pool.Fori(0, GROUPS // 2 - 1) as i:
                for p in range(2):
                    pool_phase0(2 * i + p, p)

            def max_parts(b, q):
                pool.wait_ge(max_ready, QUADS * (b + 1))
                nc.gpsimd.tensor_tensor(nmp[:, q, 0, :], nm[:, q, :], zeros[:, :], ALU.add).then_inc(nm_step, 1)
                pool.wait_ge(nm_step, 3 * b + 1)
                nc.gpsimd.tensor_tensor(nmr[:, :], nm[:, q, :], nmp[:, q, 0, :], ALU.subtract).then_inc(nm_step, 1)
                nc.gpsimd.tensor_tensor(nmp[:, q, 1, :], nm[:, q, :], nmp[:, q, 0, :], ALU.subtract).then_inc(nm_step, 1)
                pool.wait_ge(nm_step, 3 * b + 3)
                nc.gpsimd.tensor_tensor(nmp[:, q, 2, :], nmr[:, :], nmp[:, q, 1, :], ALU.subtract).then_inc(nm_ready, 1)

            max_parts(0, 0)
            max_parts(1, 1)

            def pool_attention(it, k, last):
                u = SLOTS * it + k
                pool.wait_ge(at_ready, u + 1 + SPARE)
                pool.wait_ge(att_done, u + SPARE)
                la = alt[:, 0:SPLIT_ROWS].rearrange("p (r w) -> p r w", w=LEFT)
                v = at[:, P:D]
                nc.gpsimd.tensor_tensor(la[:, 0:3], v[:, None, :].to_broadcast([P, 3, LEFT]),
                                        zeros[:, None, :].to_broadcast([P, 3, LEFT]), ALU.add).then_inc(alt_step, 1)
                pool.wait_ge(alt_step, 2 * u + 1)
                nc.gpsimd.tensor_tensor(alr[:, :], v, la[:, 0], ALU.subtract).then_inc(alt_step, 1)
                nc.gpsimd.tensor_tensor(la[:, 3:5], v[:, None, :].to_broadcast([P, 2, LEFT]),
                                        la[:, 0:1].to_broadcast([P, 2, LEFT]), ALU.subtract).then_inc(alt_ready, 1)
                pool.wait_ge(alt_step, 2 * u + 2)
                pool.wait_ge(alt_ready, 2 * u + 1)
                nc.gpsimd.tensor_tensor(la[:, 5], alr[:, :], la[:, 3], ALU.subtract).then_inc(alt_ready, 1)
                if k + 2 < SLOTS or not last:
                    pool.wait_ge(nmt_done, u + 1)
                    max_parts(u + 2, k % 2)
                pool.wait_ge(pr_ready, u + 1 + SPARE)
                pool.wait_ge(xr_in[k], 16 * (it + 1))
                nc.gpsimd.tensor_tensor(x1[:, bass.ds(u, 1)].rearrange("p o d -> p (o d)"), pr[:, :], xr[:, k],
                                        ALU.add).then_inc(x1_ready, 1)

            with pool.Fori(0, B // SLOTS - 1) as i:
                for k in range(SLOTS):
                    pool_attention(i, k, False)
            for k in range(SLOTS):
                pool_attention(B // SLOTS - 1, k, True)

            def rstd2(g, p):
                pool.wait_ge(mv2_ready, GB * (g + 1))
                nc.gpsimd.tensor_tensor(ve2[:, p], mv2[:, p, :, 1], epsilon[:, :], ALU.add).then_inc(ve2_ready, 1)
                pool.wait_ge(ve2_ready, g + 1)
                nc.gpsimd.tensor_tensor(rs2[:, p], ve2[:, p], mhalf[:, 0:GB], ALU.pow).then_inc(rs2_ready, 1)

            def residual2(it, p):
                g = 2 * it + p
                for b in range(GB):
                    pool.wait_ge(fr_ready, GB * g + b + 1 + SPARE)
                    pool.wait_ge(y_out[p], 16 * it + SPARE)
                    nc.gpsimd.tensor_tensor(yo[:, p, b], fr[:, p, b],
                                            x1[:, bass.ds(g * GB + b, 1)].rearrange("p o d -> p (o d)"),
                                            ALU.add).then_inc(y_ready, 1)

            for g in range(2):
                rstd2(g, g)
                left_parts(1, g, g)
            with pool.Fori(0, GROUPS // 2 - 1) as i:
                for p in range(2):
                    g = 2 * i + p
                    rstd2(g + 2, p)
                    pool.wait_ge(xt_done[1], g + 1)
                    left_parts(1, g + 2, p)
                    residual2(i, p)
            for p in range(2):
                residual2(GROUPS // 2 - 1, p)

        @block.scalar
        def _(act):
            for s in (v_copied, ex_ready, ot_copied, att_copied, g_ready):
                act.sem_inc(s, SPARE)
            act.wait_ge(cond_in, 16)
            nc.scalar.activation(ce[:, :], cs[:, :], ACT.Exp, scale=-1.0).then_inc(silu_exp, 1)
            act.wait_ge(ada_done, 1)
            for q in range(4):
                nc.scalar.activation(mod[:, q, :], bank[2][:, q * B:(q + 1) * B], ACT.Copy, bias=float(q % 2))\
                    .then_inc(mod_ready, 1)

            def modulate(ph, g, p):
                act.wait_ge(xt_done[ph], g + 1)
                for b in range(GB):
                    s = bass.ds(g * GB + b, 1)
                    ins = nc.scalar.activation(ht[:, p, b * N:(b + 1) * N], bank[0][:, b * N:(b + 1) * N], ACT.Identity,
                                               bias=mod[:, 2 * ph, s], scale=mod[:, 2 * ph + 1, s])
                    ins.then_inc(ht_ready[ph], 1)

            act.wait_ge(mod_ready, 4)
            modulate(0, 0, 0)

            def act_phase0(it, p, last):
                g = 2 * it + p
                if not last:
                    modulate(0, g + 1, 1 - p)
                act.wait_ge(parts_out[p], 64 * it + SPARE)
                for c in range(QKC):
                    act.wait_ge(qk_done, QKC * g + c + 1)
                    nc.scalar.activation(qkp[:, p, 0, c, :], bank[2 + c][0:QKR, 0:GT], ACT.Copy).then_inc(hi_ready, 1)
                act.wait_ge(v_done, g + 1)
                nc.scalar.activation(v_all[:, bass.ds(g * GB, GB), :, 0:HD].rearrange("p b h d -> p (b h) d"),
                                     bank[5][:, 0:GB * D].rearrange("p (k d) -> p k d", d=HD),
                                     ACT.Copy).then_inc(v_copied, 1)
                for c in range(QKC):
                    act.wait_ge(rest_ready, QKC * g + c + 1 + SPARE)
                    nc.scalar.activation(qkp[:, p, 1, c, :], qkr[:, p, c, :], ACT.Copy).then_inc(mid_ready, 1)

            with act.Fori(0, GROUPS // 2 - 1) as i:
                for p in range(2):
                    act_phase0(i, p, False)
            act_phase0(GROUPS // 2 - 1, 0, False)
            act_phase0(GROUPS // 2 - 1, 1, True)

            def nmt_copy(b):
                act.wait_ge(nmt_done, b + 1)
                nc.scalar.activation(nmt[:, :], bank[7][0:PARTS * H, 0:N // 2].bitcast(BF16), ACT.Copy)\
                    .then_inc(nmt_copied, 1)

            nmt_copy(0)

            def act_attention(it, k, last):
                u = SLOTS * it + k
                for i in range(QUADS):
                    act.wait_ge(st_done, QUADS * u + i + 1 + SPARE)
                    act.wait_ge(pv_done, QUADS * (u - 1) + i + 1 + SPARE)
                    nc.scalar.activation(ex[:, i, :], bank[2 + i % 2][:, :], ACT.Exp, scale=SCALE).then_inc(ex_ready, 1)
                    if i == 1 and (k + 1 < SLOTS or not last):
                        act.wait_ge(max_in, 16 * (u + 1))
                        nmt_copy(u + 1)
                act.wait_ge(pv_done, QUADS * (u + 1) + SPARE)
                act.wait_ge(on_done, u + SPARE)
                nc.scalar.activation(ot[:, :], bank[4][:, :], ACT.Copy).then_inc(ot_copied, 1)
                act.wait_ge(att_done, u + 1 + SPARE)
                act.wait_ge(proj_done, u + SPARE)
                nc.scalar.activation(att[:, :], bank[6][:, 0:N], ACT.Copy).then_inc(att_copied, 1)
                nc.scalar.activation(atl[:, :], bank[6][0:LROWS, N:N + N // 2].bitcast(BF16), ACT.Copy)\
                    .then_inc(att_copied, 1)

            with act.Fori(0, B // SLOTS - 1) as i:
                for k in range(SLOTS):
                    act_attention(i, k, False)
            for k in range(SLOTS):
                act_attention(B // SLOTS - 1, k, True)

            modulate(1, 0, 0)

            def act_mlp(g, p, last):
                for c, (_, m) in enumerate(HCH):
                    act.wait_ge(f1_done, NCH * g + c + 1)
                    act.wait_ge(f2_done, GB * (g - 1) + SPARE)
                    nc.scalar.activation(hg[0:m, p, c, :], bank[2 + c % 4][0:m, 0:GT], ACT.Gelu_apprx_tanh)\
                        .then_inc(g_ready, 1)
                    if c == 2 and not last:
                        modulate(1, g + 1, 1 - p)

            with act.Fori(0, GROUPS // 2 - 1) as i:
                for p in range(2):
                    act_mlp(2 * i + p, p, False)
            act_mlp(GROUPS - 2, 0, False)
            act_mlp(GROUPS - 1, 1, True)

        @block.vector
        def _(dve):
            for s in (lo_ready, rest_ready, pr_ready, at_ready, fr_ready):
                dve.sem_inc(s, SPARE)
            nc.vector.memset(bank[4][:, :], 0.0).then_inc(set_by_dve, 1)
            nc.vector.memset(ctl[:, :], 1.0).then_inc(silu_step, 1)
            nc.vector.memset(hg[96:97, :, NCH - 1, :], 1.0).then_inc(set_by_dve, 1)
            nc.vector.memset(kt[MAX_ROW:SROWS, :, :].bitcast(F32), BF16_ONES).then_inc(set_by_dve, 1)
            dve.wait_ge(silu_exp, 1)
            nc.vector.tensor_scalar(cr[:, :], ce[:, :], 1.0, None, ALU.add).then_inc(silu_step, 1)
            dve.wait_ge(silu_step, 2)
            nc.vector.reciprocal(ce[:, :], cr[:, :]).then_inc(silu_step, 1)
            dve.wait_ge(silu_step, 3)
            nc.vector.tensor_tensor(cr[:, :], cs[:, :], ce[:, :], ALU.mult).then_inc(silu_ready, 1)
            dve.wait_ge(ct_turned, 1)
            nc.vector.tensor_copy(ct[:, :], bank[0][:, 0:B]).then_inc(ct_copied, 1)
            nc.vector.tensor_copy(ctl[0:LEFT, :], bank[0][0:LEFT, B:2 * B]).then_inc(ct_copied, 1)
            dve.wait_ge(ada_done, 2)
            for f in range(2):
                src = bank[6 + f]
                left = 2 * f * LEFT
                nc.vector.tensor_copy(left_r[:, left:left + LEFT], src[0:B, P:D]).then_inc(rows_ready, 1)
                nc.vector.tensor_scalar(left_r[:, left + LEFT:left + 2 * LEFT], src[0:B, D + P:2 * D], 1.0, None,
                                        ALU.add).then_inc(rows_ready, 1)
                nc.vector.tensor_copy(gate_r[:, f * D:(f + 1) * D], src[0:B, 2 * D:3 * D]).then_inc(rows_ready, 1)
            for b in range(B):
                if b % 4 == 0:
                    dve.wait_ge(x_in, 64)
                nc.vector.bn_stats(st[:, b, :], xs[:, b, :]).then_inc(stat_step, 1)
            for b in range(B):
                dve.wait_ge(stat_step, b + 1)
                nc.vector.bn_aggr(mv[:, b, :], st[:, b, :]).then_inc(mv_ready, 1)

            def weight_parts(n, lo, hi):
                c = slice(lo, hi)
                nc.vector.tensor_copy(wlb[:, c], wlf[:, c]).then_inc(wl_step, 1)
                dve.wait_ge(wl_step, 3 * n + 1)
                nc.vector.scalar_tensor_tensor(out=wlr[:, c], in0=wlb[:, c], scalar=msk[:, 0:1], in1=wlf[:, c],
                                               op0=ALU.mult, op1=ALU.add).then_inc(wl_step, 1)
                dve.wait_ge(wl_step, 3 * n + 2)
                nc.vector.tensor_copy(wlb[:, c], wlr[:, c]).then_inc(wl_step, 1)
                dve.wait_ge(wl_step, 3 * n + 3)
                nc.vector.scalar_tensor_tensor(out=wl[:, c], in0=wlb[:, c], scalar=msk[:, 1:2], in1=wlr[:, c],
                                               op0=ALU.mult, op1=ALU.add).then_inc(wl_ready, 1)

            def normalise(ph, g, p):
                for b in range(GB):
                    s = bass.ds(g * GB + b, 1)
                    src = (xs, x1)[ph][:, s].rearrange("p o d -> p (o d)")
                    mean = mv[:, s, 0] if ph == 0 else mv2[:, p, b, 0:1]
                    rstd = rs[:, s] if ph == 0 else rs2[:, p, b:b + 1]
                    ins = nc.vector.tensor_scalar(xn[:, p, b, :], src, mean, rstd, ALU.subtract, ALU.mult)
                ins.then_inc(xn_ready[ph], 1)

            def left_copy(ph, g, p):
                dve.wait_ge(xt_done[ph], g + 1)
                nc.vector.tensor_copy(hl[:, p, :], bank[1][0:LROWS, 0:GT // 2].bitcast(BF16)).then_inc(hl_ready[ph], 1)

            dve.wait_ge(rs_ready, 1)
            normalise(0, 0, 0)
            normalise(0, 1, 1)
            dve.wait_ge(wl_in, 48)
            weight_parts(0, 0, C_P)
            weight_parts(1, C_P, WCOLS)
            left_copy(0, 0, 0)

            def dve_phase0(g, p, more, last):
                if more:
                    dve.wait_ge(xt_done[0], g + 1)
                    normalise(0, g + 2, p)
                if not last:
                    left_copy(0, g + 1, 1 - p)
                dve.wait_ge(lo_ready, QKC * (g - 1) + SPARE)
                for c in range(QKC):
                    dve.wait_ge(hi_ready, QKC * g + c + 1)
                    nc.vector.tensor_tensor(qkr[:, p, c, :], bank[2 + c][0:QKR, 0:GT], qkp[:, p, 0, c, :],
                                            ALU.subtract).then_inc(rest_ready, 1)
                for c in range(QKC):
                    dve.wait_ge(mid_ready, QKC * g + c + 1)
                    nc.vector.tensor_tensor(qkp[:, p, 2, c, :], qkr[:, p, c, :], qkp[:, p, 1, c, :],
                                            ALU.subtract).then_inc(lo_ready, 1)

            with dve.Fori(0, GROUPS // 2 - 1) as i:
                for p in range(2):
                    dve_phase0(2 * i + p, p, True, False)
            dve_phase0(GROUPS - 2, 0, False, False)
            dve_phase0(GROUPS - 1, 1, False, True)

            def negated_max(b, q, i):
                dve.wait_ge(s_done, QUADS * b + i + 1)
                nc.vector.tensor_reduce(nm[:, q, 4 * i:4 * i + 4], bank[i % 2][:, :].rearrange("p (h m) -> p h m", h=4),
                                        AX.X, ALU.max, negate=True).then_inc(max_ready, 1)

            for b in range(2):
                for i in range(QUADS):
                    negated_max(b, b, i)

            def dve_attention(it, k, last):
                u = SLOTS * it + k
                scores = k + 2 < SLOTS or not last
                if scores:
                    dve.wait_ge(nm_ready, u + 1)
                    negated_max(u + 2, k % 2, 0)
                    negated_max(u + 2, k % 2, 1)
                heads = bank[5][:, :].rearrange("p (h w) -> p h w", h=H)
                dve.wait_ge(on_done, u + 1 + SPARE)
                nc.vector.reciprocal(rd[:, :], heads[:, :, HD]).then_inc(rd_ready, 1)
                dve.wait_ge(rd_ready, u + 1)
                dve.wait_ge(att_done, u + SPARE)
                nc.vector.tensor_tensor(at[:, :].rearrange("p (h d) -> p h d", h=H), heads[:, :, 0:HD],
                                        rd[:, :, None].to_broadcast([P, H, HD]), ALU.mult).then_inc(at_ready, 1)
                if scores:
                    negated_max(u + 2, k % 2, 2)
                    negated_max(u + 2, k % 2, 3)
                dve.wait_ge(proj_done, u + 1 + SPARE)
                dve.wait_ge(x1_ready, u + SPARE)
                nc.vector.tensor_tensor(pr[:, :], bank[7][:, 0:D], gates[:, bass.ds(u, 1), 0:D].rearrange("p o d -> p (o d)"),
                                        ALU.mult).then_inc(pr_ready, 1)

            dve.wait_ge(gates_in, 16)
            with dve.Fori(0, B // SLOTS - 1) as i:
                for k in range(SLOTS):
                    dve_attention(i, k, False)
            for k in range(SLOTS):
                dve_attention(B // SLOTS - 1, k, True)

            def statistics2(g, p):
                for b in range(GB):
                    dve.wait_ge(x1_ready, GB * g + b + 1 + SPARE)
                    nc.vector.bn_stats(st2[:, p, b, :], x1[:, bass.ds(g * GB + b, 1)].rearrange("p o d -> p (o d)"))\
                        .then_inc(st2_done, 1)
                dve.wait_ge(st2_done, GB * (g + 1))
                dve.sem_inc(passed, 1)
                for b in range(GB):
                    nc.vector.bn_aggr(mv2[:, p, b, :], st2[:, p, b, :]).then_inc(mv2_ready, 1)

            def gate2(g, p):
                for b in range(GB):
                    dve.wait_ge(f2_done, GB * g + b + 1 + SPARE)
                    dve.wait_ge(y_ready, GB * (g - 1) + SPARE)
                    nc.vector.tensor_tensor(fr[:, p, b, :], bank[6 + b][:, 0:D],
                                            gates[:, bass.ds(g * GB + b, 1), D:2 * D].rearrange("p o d -> p (o d)"),
                                            ALU.mult).then_inc(fr_ready, 1)

            for g in range(2):
                statistics2(g, g)
            for g in range(2):
                dve.wait_ge(rs2_ready, g + 1)
                normalise(1, g, g)
            left_copy(1, 0, 0)

            def dve_mlp(g, p, more, last):
                if more:
                    statistics2(g + 2, p)
                    dve.wait_ge(rs2_ready, g + 3)
                    dve.wait_ge(xt_done[1], g + 1)
                    normalise(1, g + 2, p)
                if not last:
                    left_copy(1, g + 1, 1 - p)
                gate2(g, p)

            with dve.Fori(0, GROUPS // 2 - 1) as i:
                for p in range(2):
                    dve_mlp(2 * i + p, p, True, False)
            dve_mlp(GROUPS - 2, 0, False, False)
            dve_mlp(GROUPS - 1, 1, False, True)

        @block.tensor
        def _(pe):
            for s in (pv_done, st_done, on_done, att_done, proj_done, f2_done):
                pe.sem_inc(s, SPARE)
            pe.wait_ge(consts, 2)
            pe.wait_ge(silu_ready, 1)
            nc.tensor.transpose(bank[0][:, 0:B], cr[:, 0:P], ident[0:B, 0:B])
            nc.tensor.transpose(bank[0][0:LEFT, B:2 * B], cr[:, P:D], ident[0:B, 0:B]).then_inc(ct_turned, 1)
            pe.wait_ge(ct_copied, 2)
            pe.wait_ge(wa_in, 32)
            for n, q in enumerate((0, 1, 3, 4)):
                dst = bank[2][:, n * B:(n + 1) * B]
                nc.tensor.matmul(dst, wa[:, q * D:q * D + P], ct[:, :], start=True, stop=False)
                mm = nc.tensor.matmul(dst, wal[:, q * D:q * D + P], ctl[:, :], start=False, stop=True)
            mm.then_inc(ada_done, 1)
            for f in range(2):
                dst, c = bank[6 + f][0:B, 0:3 * D], slice(f * 3 * D, (f + 1) * 3 * D)
                nc.tensor.matmul(dst, ct[:, :], wa[:, c], start=True, stop=False)
                mm = nc.tensor.matmul(dst, ctl[:, :], wal[:, c], start=False, stop=True)
            mm.then_inc(ada_done, 1)

            def turn(ph, g, p):
                pe.wait_ge(xn_ready[ph], g + 1)
                for b in range(GB):
                    nc.tensor.transpose(bank[0][:, b * N:(b + 1) * N], xn[:, p, b, 0:P], ident[:, :])
                pe.wait_ge(left_ready[ph], 2 * (g + 1))
                parts = bank[1][0:LROWS, 0:GT // 2].bitcast(BF16)
                for b in range(GB):
                    mm = nc.tensor.transpose(parts[:, b * N:(b + 1) * N], lt[:, p, b, :], ident_b[:, :])
                mm.then_inc(xt_done[ph], 1)

            pe.wait_ge(ones_set, 6)
            turn(0, 0, 0)
            pe.wait_ge(wm_in, 16)
            pe.wait_ge(wl_ready, 2)
            pe.wait_ge(mod_ready, 4)
            pe.wait_ge(cleared, 2)
            pe.wait_ge(set_by_dve, 3)

            def pe_phase0(g, p, last):
                if not last:
                    pe.wait_ge(ht_ready[0], GB * (g + 1))
                    pe.wait_ge(hl_ready[0], g + 1)
                    turn(0, g + 1, 1 - p)
                else:
                    pe.wait_ge(ht_ready[0], GB * (g + 1))
                    pe.wait_ge(hl_ready[0], g + 1)
                for c in range(QKC):
                    pe.wait_ge(rest_ready, QKC * (g - 1) + c + 1 + SPARE)
                    w = slice(c * QKR, (c + 1) * QKR)
                    dst = bank[2 + c][0:QKR, 0:GT]
                    nc.tensor.matmul(dst, wm[:, w], ht[:, p, :], start=True, stop=False)
                    nc.tensor.matmul(dst, wl[:, w], hl[:, p, :], start=False, stop=True).then_inc(qk_done, 1)
                pe.wait_ge(v_copied, g + SPARE)
                for b in range(GB):
                    dst, t = bank[5][:, b * D:(b + 1) * D], slice(b * N, (b + 1) * N)
                    nc.tensor.matmul(dst, ht[:, p, t], wm[:, C_V:C_P], start=True, stop=False)
                    mm = nc.tensor.matmul(dst, hl[:, p, t], wl[:, C_V:C_P], start=False, stop=True)
                mm.then_inc(v_done, 1)

            with pe.Fori(0, GROUPS // 2 - 1) as i:
                for p in range(2):
                    pe_phase0(2 * i + p, p, False)
            pe_phase0(GROUPS - 2, 0, False)
            pe_phase0(GROUPS - 1, 1, True)

            def scores_q(b, slot, i):
                for j in range(4):
                    mm = nc.tensor.matmul(bank[i % 2][:, j * N:(j + 1) * N], qt[0:MAX_ROW, slot, head(i, j)],
                                          kt[0:MAX_ROW, slot, head(i, j)], start=True, stop=True)
                mm.then_inc(s_done, 1)

            def scores_k(slot, i):
                for j in range(4):
                    mm = nc.tensor.matmul(bank[2 + i % 2][:, j * N:(j + 1) * N], kt[0:SROWS, slot, head(i, j)],
                                          qt[0:SROWS, slot, head(i, j)], start=True, stop=True)
                mm.then_inc(st_done, 1)

            def values(slot, i):
                for j in range(4):
                    mm = nc.tensor.matmul(bank[4][32 * j:32 * j + VW, i * N:(i + 1) * N], vt[:, slot, 4 * i + j, :],
                                          ex[:, i, j * N:(j + 1) * N], start=True, stop=True)
                mm.then_inc(pv_done, 1)

            def turn_max(q):
                pe.sem_inc(passed, 1)
                nc.tensor.transpose(bank[7][0:PARTS * H, 0:N // 2].bitcast(BF16),
                                    nmp[:, q].rearrange("p l h -> p (l h)"), ident_b[:, :]).then_inc(nmt_done, 1)

            pe.wait_ge(cleared, 2)
            pe.wait_ge(set_by_dve, 3)
            for b in range(2):
                pe.wait_ge(qk_in[b], 32)
                for i in range(QUADS):
                    if b + i // 2 > 0:
                        pe.wait_ge(max_ready, QUADS * b + i - 1)
                    scores_q(b, b, i)
            pe.wait_ge(nm_ready, 1)
            turn_max(0)
            pe.wait_ge(rest_ready, QKC * GROUPS + SPARE)
            pe.wait_ge(v_copied, GROUPS + SPARE)

            def pe_attention(it, k, last):
                u = SLOTS * it + k
                k2 = (k + 2) % SLOTS
                scores = k + 2 < SLOTS or not last

                def keys(i):
                    pe.wait_ge(ex_ready, QUADS * u + i - 1 + SPARE)
                    scores_k(k, i)

                def pv(i):
                    pe.wait_ge(ex_ready, QUADS * u + i + 1 + SPARE)
                    values(k, i)

                def queries(i):
                    if scores:
                        pe.wait_ge(max_ready, QUADS * (u + 2) + i - 1)
                        scores_q(u + 2, k2, i)

                pe.wait_ge(max_in, 16 * (u + 1))
                keys(0)
                keys(1)
                pe.wait_ge(v_in[k], 16 * (it + 1))
                pe.wait_ge(ot_copied, u + SPARE)
                pv(0)
                if k + 1 < SLOTS or not last:
                    pe.wait_ge(nm_ready, u + 2)
                    pe.wait_ge(pr_ready, u + SPARE)
                    turn_max((k + 1) % 2)
                keys(2)
                pv(1)
                keys(3)
                pv(2)
                if scores:
                    pe.wait_ge(qk_in[k2], 32 * (it + 1 + (k + 2) // SLOTS))
                queries(0)
                pv(3)
                queries(1)
                pe.wait_ge(ot_copied, u + 1 + SPARE)
                pe.wait_ge(at_ready, u + SPARE)
                for i in range(QUADS):
                    mm = nc.tensor.transpose(bank[5][:, i * N:(i + 1) * N], ot[:, i * N:(i + 1) * N], ident[:, :])
                mm.then_inc(on_done, 1)
                queries(2)
                pe.wait_ge(at_ready, u + 1 + SPARE)
                pe.wait_ge(alt_ready, 2 * (u + 1))
                pe.wait_ge(att_copied, 2 * u + SPARE)
                nc.tensor.transpose(bank[6][:, 0:N], at[:, 0:P], ident[:, :])
                nc.tensor.transpose(bank[6][0:LROWS, N:N + N // 2].bitcast(BF16), alt[:, :], ident_b[:, :])\
                    .then_inc(att_done, 1)
                queries(3)
                pe.wait_ge(att_copied, 2 * (u + 1) + SPARE)
                if k + 1 < SLOTS or not last:
                    pe.wait_ge(nmt_copied, u + 2)
                nc.tensor.matmul(bank[7][:, 0:D], att[:, :], wm[:, C_P:C_F], start=True, stop=False)
                nc.tensor.matmul(bank[7][:, 0:D], atl[:, :], wl[:, C_P:C_F], start=False, stop=True).then_inc(proj_done, 1)

            pe.wait_ge(wrest_in, 16)
            with pe.Fori(0, B // SLOTS - 1) as i:
                for k in range(SLOTS):
                    pe_attention(i, k, False)
            for k in range(SLOTS):
                pe_attention(B // SLOTS - 1, k, True)

            turn(1, 0, 0)
            pe.wait_ge(w2_in, 48)
            pe.wait_ge(pr_ready, B + SPARE)

            def pe_mlp(g, p, last):
                def hidden(c):
                    before = NCH * g if c == 0 else NCH * g + 1 if c == 4 else NCH * (g - 1) + c + 1
                    pe.wait_ge(g_ready, before + SPARE)
                    h0, m = HCH[c]
                    w = slice(C_F + h0, C_F + h0 + m)
                    dst = bank[2 + c % 4][0:m, 0:GT]
                    nc.tensor.matmul(dst, wm[:, w], ht[:, p, :], start=True, stop=False)
                    nc.tensor.matmul(dst, wl[:, w], hl[:, p, :], start=False, stop=True).then_inc(f1_done, 1)

                pe.wait_ge(ht_ready[1], GB * (g + 1))
                pe.wait_ge(hl_ready[1], g + 1)
                for c in range(3):
                    hidden(c)
                if not last:
                    turn(1, g + 1, 1 - p)
                hidden(3)
                hidden(4)
                for b in range(GB):
                    pe.wait_ge(fr_ready, GB * (g - 1) + b + 1 + SPARE)
                    for c, (_, m) in enumerate(HCH):
                        rows = m + (c == NCH - 1)
                        if b == 0:
                            pe.wait_ge(g_ready, NCH * g + c + 1 + SPARE)
                        mm = nc.tensor.matmul(bank[6 + b][:, 0:D], hg[0:rows, p, c, b * N:(b + 1) * N],
                                              w2[0:rows, c, :], start=(c == 0), stop=(c == NCH - 1))
                    mm.then_inc(f2_done, 1)

            with pe.Fori(0, GROUPS // 2 - 1) as i:
                for p in range(2):
                    pe_mlp(2 * i + p, p, False)
            pe_mlp(GROUPS - 2, 0, False)
            pe_mlp(GROUPS - 1, 1, True)


def part_masks():
    part = np.array([n for m in range(PARTS) for n in range(PARTS - m) for _ in range(LEFT)] + list(range(PARTS)))
    return np.stack([-(part > 0).astype(np.float32), -(part > 1).astype(np.float32)], axis=1)


def kernel(x, cond_1152, L0_cond_w_qkv, L0_cond_b_qkv, L0_cond_w_proj, L0_cond_b_proj, L0_cond_w_fc1,
           L0_cond_b_fc1, L0_cond_w_fc2, L0_cond_b_fc2, L0_cond_w_ada, L0_cond_b_ada):
    from concourse import bacc
    from concourse.bass_utils import run_bass_kernel_spmd

    def with_bias(w, b):
        return np.concatenate([np.asarray(w), np.asarray(b)[None]], axis=0)

    qkv = with_bias(L0_cond_w_qkv, L0_cond_b_qkv)
    qk = qkv[:, 0:2 * D].reshape(D + 1, 2, H, QKC, HD // QKC).transpose(0, 3, 4, 1, 2).reshape(D + 1, 2 * D)
    arrays = {
        "x": np.asarray(x),
        "cond": np.asarray(cond_1152),
        "w_all": np.concatenate([qk, qkv[:, 2 * D:], with_bias(L0_cond_w_proj, L0_cond_b_proj),
                                 with_bias(L0_cond_w_fc1, L0_cond_b_fc1)], axis=1),
        "w_fc2": with_bias(L0_cond_w_fc2, L0_cond_b_fc2),
        "w_ada": with_bias(L0_cond_w_ada, L0_cond_b_ada),
        "masks": part_masks(),
    }
    arrays = {f"in_{k}": np.ascontiguousarray(a) for k, a in arrays.items()}
    nc = bacc.Bacc("TRN2", target_bir_lowering=False, num_devices=1)
    args = [nc.dram_tensor(k, a.shape, mybir.dt.from_np(a.dtype), kind="ExternalInput").ap() for k, a in arrays.items()]
    args.append(nc.dram_tensor("out_x", (B, N, D), F32, kind="ExternalOutput").ap())
    build(nc, *args)
    result = run_bass_kernel_spmd(nc, [arrays], core_ids=[0])
    return result.results[0]["out_x"]
```

```python
from contextlib import ExitStack

import numpy as np

import concourse.bass as bass
from concourse import mybir

F32 = mybir.dt.float32
BF16 = mybir.dt.bfloat16
ACT = mybir.ActivationFunctionType
ALU = mybir.AluOpType
AX = mybir.AxisListType

B, N, D, H = 16, 128, 144, 16
HD = D // H
HID = 4 * D
P = 128
EPS = 1e-6
SCALE = float(HD) ** -0.5
LEFT = D - P
PARTS = 3
SPLIT_ROWS = 6 * LEFT
LROWS = SPLIT_ROWS + PARTS
GB = 2
GT = GB * N
GROUPS = B // GB
QKC = 3
QKR = 2 * D // QKC
PROD_ROWS = PARTS * PARTS * HD
MAX_ROW = 96
SROWS = MAX_ROW + PARTS
QUADS = H // 4
VW = HD + 1
SLOTS = 4
HCH = [(0, 128), (128, 128), (256, 128), (384, 96), (480, 96)]
NCH = len(HCH)
WCOLS = 3 * D + D + HID
C_V, C_P, C_F = 2 * D, 3 * D, 4 * D
BF16_ONES = float(np.array([0x3F803F80], np.uint32).view(np.float32)[0])
SPARE = 128


def build(nc, x, cond, w_all, w_fc2, w_ada, masks, out):
    ctx = ExitStack()
    with ctx:
        def sb(name, shape, dt=F32):
            return ctx.enter_context(nc.sbuf_tensor(name, shape, dt))

        def sem(name):
            return ctx.enter_context(nc.semaphore(name))

        bank = [ctx.enter_context(nc.psum_tensor(f"bank{i}", [P, 512], F32)) for i in range(8)]

        parts_d = nc.dram_tensor("parts_d", [B, PARTS + 2, HD, 2, H, N], BF16, kind="Internal").ap()
        left_d = nc.dram_tensor("left_d", [B, 4 * LEFT], F32, kind="Internal").ap()
        gate_d = nc.dram_tensor("gate_d", [B, 2 * D], F32, kind="Internal").ap()

        ident = sb("ident", [P, P])
        ident_b = sb("ident_b", [P, P], BF16)
        zeros = sb("zeros", [P, H])
        epsilon = sb("epsilon", [P, GB])
        mhalf = sb("mhalf", [P, B])
        msk = sb("msk", [LROWS, 2])
        wm = sb("wm", [P, WCOLS])
        wl = sb("wl", [LROWS, WCOLS], BF16)
        wlf = sb("wlf", [LROWS, WCOLS])
        wlr = sb("wlr", [LROWS, WCOLS])
        wlb = sb("wlb", [LROWS, WCOLS], BF16)
        w2 = sb("w2", [P, NCH, D])
        wa = sb("wa", [P, 6 * D])
        wal = sb("wal", [LEFT + 1, 6 * D])
        cs = sb("cs", [B, D])
        ce = sb("ce", [B, D])
        cr = sb("cr", [B, D])
        ct = sb("ct", [P, B])
        ctl = sb("ctl", [LEFT + 1, B])
        mod = sb("mod", [P, 4, B])
        left_r = sb("left_r", [B, 4 * LEFT])
        gate_r = sb("gate_r", [B, 2 * D])
        bl = sb("bl", [P, B, 4 * LEFT])
        gates = sb("gates", [P, B, 2 * D])
        xs = sb("xs", [P, B, D])
        x1 = sb("x1", [P, B, D])
        st = sb("st", [P, B, 6])
        mv = sb("mv", [P, B, 2])
        ve = sb("ve", [P, B])
        rs = sb("rs", [P, B])
        st2 = sb("st2", [P, 2, GB, 6])
        mv2 = sb("mv2", [P, 2, GB, 2])
        ve2 = sb("ve2", [P, 2, GB])
        rs2 = sb("rs2", [P, 2, GB])
        xn = sb("xn", [P, 2, GB, D])
        lm = sb("lm", [P, GB, LEFT])
        lv = sb("lv", [P, GB, LEFT])
        lr = sb("lr", [P, GB, LEFT])
        lt = sb("lt", [P, 2, GB, LROWS], BF16)
        ht = sb("ht", [P, 2, GT])
        hl = sb("hl", [LROWS, 2, GT], BF16)
        qkp = sb("qkp", [QKR, 2, PARTS, QKC, GT], BF16)
        qkr = sb("qkr", [QKR, 2, QKC, GT])
        v_all = sb("v_all", [P, B, H, VW])
        qt = sb("qt", [P, SLOTS, H * N], BF16)
        kt = sb("kt", [P, SLOTS, H * N], BF16)
        vt = sb("vt", [P, SLOTS, H, VW])
        nm = sb("nm", [P, 2, H])
        nmr = sb("nmr", [P, H])
        nmp = sb("nmp", [P, PARTS, H], BF16)
        nmt = sb("nmt", [PARTS * H, N], BF16)
        ex = sb("ex", [P, QUADS, 4 * N])
        ot = sb("ot", [P, QUADS * N])
        rd = sb("rd", [P, H])
        at = sb("at", [P, D])
        alr = sb("alr", [P, LEFT])
        alt = sb("alt", [P, LROWS], BF16)
        att = sb("att", [P, N])
        atl = sb("atl", [LROWS, N], BF16)
        pr = sb("pr", [P, D])
        hg = sb("hg", [P, 2, NCH, GT])
        fr = sb("fr", [P, 2, GB, D])
        yo = sb("yo", [P, 2, GB, D])

        passed = sem("passed")
        cond_in, wa_in, wm_in, wrest_in, wl_in, w2_in, x_in = (sem(n) for n in (
            "cond_in", "wa_in", "wm_in", "wrest_in", "wl_in", "w2_in", "x_in"))
        consts, ident_zero, cleared, set_by_dve = sem("consts"), sem("ident_zero"), sem("cleared"), sem("set_by_dve")
        silu_exp, silu_step, silu_ready = sem("silu_exp"), sem("silu_step"), sem("silu_ready")
        ct_turned, ct_copied, ada_done, mod_ready = sem("ct_turned"), sem("ct_copied"), sem("ada_done"), sem("mod_ready")
        rows_ready, rows_out, bl_in, gates_in = sem("rows_ready"), sem("rows_out"), sem("bl_in"), sem("gates_in")
        wl_step, wl_ready = sem("wl_step"), sem("wl_ready")
        stat_step, mv_ready, ve_ready, rs_ready = sem("stat_step"), sem("mv_ready"), sem("ve_ready"), sem("rs_ready")
        xn_ready = [sem("xn_ready0"), sem("xn_ready2")]
        left_step = [sem("left_step0"), sem("left_step2")]
        left_ready = [sem("left_ready0"), sem("left_ready2")]
        xt_done = [sem("xt_done0"), sem("xt_done2")]
        ht_ready = [sem("ht_ready0"), sem("ht_ready2")]
        hl_ready = [sem("hl_ready0"), sem("hl_ready2")]
        qk_done, hi_ready, rest_ready, mid_ready, lo_ready = (sem(n) for n in (
            "qk_done", "hi_ready", "rest_ready", "mid_ready", "lo_ready"))
        v_done, v_copied, ones_set = sem("v_done"), sem("v_copied"), sem("ones_set")
        parts_out = [sem(f"parts_out{p}") for p in range(2)]
        qk_in, v_in = ([sem(f"{n}{k}") for k in range(SLOTS)] for n in ("qk_in", "v_in"))
        max_in = sem("max_in")
        s_done, max_ready, nm_step, nm_ready = sem("s_done"), sem("max_ready"), sem("nm_step"), sem("nm_ready")
        nmt_done, nmt_copied = sem("nmt_done"), sem("nmt_copied")
        st_done, ex_ready, pv_done, ot_copied = sem("st_done"), sem("ex_ready"), sem("pv_done"), sem("ot_copied")
        on_done, rd_ready, at_ready = sem("on_done"), sem("rd_ready"), sem("at_ready")
        alt_step, alt_ready, att_done, att_copied = sem("alt_step"), sem("alt_ready"), sem("att_done"), sem("att_copied")
        proj_done, pr_ready, x1_ready = sem("proj_done"), sem("pr_ready"), sem("x1_ready")
        st2_done, mv2_ready, ve2_ready, rs2_ready = sem("st2_done"), sem("mv2_ready"), sem("ve2_ready"), sem("rs2_ready")
        f1_done, g_ready, f2_done, fr_ready, y_ready = (sem(n) for n in (
            "f1_done", "g_ready", "f2_done", "fr_ready", "y_ready"))
        y_out = [sem(f"y_out{p}") for p in range(2)]

        block = ctx.enter_context(nc.Block())

        x_tok = x.rearrange("b n d -> n b d")
        out_tok = out.rearrange("b n d -> n b d")

        def head(i, j):
            h = 4 * i + j
            return slice(h * N, (h + 1) * N)

        def units(engine, unit):
            unit(0, 0, 0)
            with engine.Fori(0, B // SLOTS - 1) as it:
                for k in range(SLOTS):
                    unit(SLOTS * it + 1 + k, 1 + k, it)
            for k in range(SLOTS - 1):
                unit(B - SLOTS + 1 + k, 1 + k, B // SLOTS - 1)

        def ahead(u, n):
            return not isinstance(u, int) or u + n < B

        @block.sync
        def _(sp):
            for s in (*parts_out, *y_out):
                sp.sem_inc(s, SPARE)
            sp.dma_start(cs[:, :], cond).then_inc(cond_in, 16)
            sp.dma_start(wa[:, :], w_ada[0:P, :]).then_inc(wa_in, 16)
            sp.dma_start(wal[:, :], w_ada[P:D + 1, :]).then_inc(wa_in, 16)
            for q in range(4):
                sp.dma_start(xs[:, 4 * q:4 * q + 4, :], x_tok[:, 4 * q:4 * q + 4, :]).then_inc(x_in, 16)
            sp.dma_start(msk[:, :], masks).then_inc(wl_in, 16)
            lrows, brow = w_all[P:D, :], w_all[D:D + 1, :]
            sp.dma_start(wlf[0:SPLIT_ROWS, :], bass.AP(tensor=lrows.tensor, offset=lrows.offset,
                         ap=[[0, 6], [WCOLS, LEFT], [1, WCOLS]])).then_inc(wl_in, 16)
            sp.dma_start(wlf[SPLIT_ROWS:LROWS, :], bass.AP(tensor=brow.tensor, offset=brow.offset,
                         ap=[[0, PARTS], [1, WCOLS]])).then_inc(wl_in, 16)
            sp.dma_start(wm[:, 0:C_P], w_all[0:P, 0:C_P]).then_inc(wm_in, 16)
            sp.wait_ge(rows_ready, 6)
            sp.dma_start(left_d, left_r[:, :]).then_inc(rows_out, 16)
            sp.dma_start(gate_d, gate_r[:, :]).then_inc(rows_out, 16)
            sp.wait_ge(rows_out, 32)
            sp.dma_start(bl[:, :, :], bass.AP(tensor=left_d.tensor, offset=left_d.offset,
                         ap=[[0, P], [1, B * 4 * LEFT]])).then_inc(bl_in, 16)
            sp.dma_start(wm[:, C_P:WCOLS], w_all[0:P, C_P:WCOLS]).then_inc(wrest_in, 16)
            sp.dma_start(gates[:, :, :], bass.AP(tensor=gate_d.tensor, offset=gate_d.offset,
                         ap=[[0, P], [1, B * 2 * D]])).then_inc(gates_in, 16)
            sp.dma_start(w2[:, 0:3, :], w_fc2[0:3 * P, :].rearrange("(c p) n -> p c n", p=P)).then_inc(w2_in, 16)
            sp.dma_start(w2[0:96, 3, :], w_fc2[HCH[3][0]:HCH[4][0], :]).then_inc(w2_in, 16)
            sp.dma_start(w2[0:97, 4, :], w_fc2[HCH[4][0]:HID + 1, :]).then_inc(w2_in, 16)

            def parts_store(g, p):
                sp.wait_ge(lo_ready, QKC * (g + 1) + SPARE)
                for b in range(GB):
                    dst = parts_d[bass.ds(g * GB + b, 1)].rearrange("o l (c e) a h t -> (e a h) (o l c) t", c=QKC)
                    src = qkp[:, p, :, :, b * N:(b + 1) * N].rearrange("p l c t -> p (l c) t")
                    sp.dma_start(dst[:, 0:PARTS * QKC], src).then_inc(parts_out[p], 16)
                    sp.dma_start(dst[:, PARTS * QKC:(PARTS + 2) * QKC], src[:, 0:2 * QKC]).then_inc(parts_out[p], 16)

            with sp.Fori(0, GROUPS // 2) as i:
                for p in range(2):
                    parts_store(2 * i + p, p)

            def qk_load(b, slot):
                k = parts_d[bass.ds(b, 1), 0:PARTS, :, 1].rearrange("o l d h t -> (o l d) (h t)")
                q = parts_d[bass.ds(b, 1), 0:PARTS, :, 0].rearrange("o l d h t -> (o l d) (h t)")
                row, block_of = 2 * H * N, HD * 2 * H * N
                for tile, a, rot in ((kt, k, 0), (qt, q, block_of)):
                    src = bass.AP(tensor=a.tensor, offset=a.offset, ap=[[row, PARTS * HD], [rot, PARTS], [1, H * N]])
                    sp.dma_start(tile[0:PROD_ROWS, slot, :], src).then_inc(qk_in[slot], 16)

            def v_load(b, slot):
                sp.dma_start(vt[:, slot], v_all[:, bass.ds(b, 1)].rearrange("p o h w -> p (o h) w")).then_inc(v_in[slot], 16)

            def max_load(b, slot):
                sp.wait_ge(nmt_copied, b + 1)
                sp.dma_start(qt[MAX_ROW:SROWS, slot, :], nmt[:, :]).then_inc(max_in, 16)

            for p in range(2):
                sp.wait_ge(parts_out[p], SPARE + 64 * GROUPS // 2)
            sp.wait_ge(cleared, 2)
            for b in range(3):
                qk_load(b, b)
            sp.wait_ge(v_copied, SPARE + GROUPS)
            for b in range(2):
                v_load(b, b)
            max_load(0, 0)

            def attention_loads(u, k, it):
                if ahead(u, 3):
                    sp.wait_ge(st_done, 4 * u + SPARE)
                    sp.sem_inc(passed, 1)
                    qk_load(u + 3, (k + 3) % SLOTS)
                if ahead(u, 1):
                    max_load(u + 1, (k + 1) % SLOTS)
                if ahead(u, 2):
                    sp.wait_ge(pv_done, 4 * (u - 1) + SPARE)
                    sp.sem_inc(passed, 1)
                    v_load(u + 2, (k + 2) % SLOTS)

            units(sp, attention_loads)

            with sp.Fori(0, GROUPS // 2) as i:
                for p in range(2):
                    g = 2 * i + p
                    sp.wait_ge(y_ready, GB * (g + 1) + SPARE)
                    sp.dma_start(out_tok[:, bass.ds(g * GB, GB), :], yo[:, p]).then_inc(y_out[p], 16)
            for p in range(2):
                sp.wait_ge(y_out[p], SPARE + 16 * GROUPS // 2)

        @block.gpsimd
        def _(pool):
            for s in (x1_ready, y_ready):
                pool.sem_inc(s, SPARE)
            nc.gpsimd.memset(ident[:, :], 0.0).then_inc(ident_zero, 1)
            nc.gpsimd.memset(ident_b[:, :], 0.0).then_inc(ident_zero, 1)
            pool.wait_ge(ident_zero, 2)
            for m in (ident, ident_b):
                nc.gpsimd.affine_select(out=m[:, :], in_=m[:, :], compare_op=ALU.not_equal, fill=1.0, base=0,
                                        pattern=[[-1, P]], channel_multiplier=1).then_inc(consts, 1)
            nc.gpsimd.memset(mhalf[:, :], -0.5).then_inc(ones_set, 1)
            nc.gpsimd.memset(zeros[:, :], 0.0).then_inc(ones_set, 1)
            nc.gpsimd.memset(epsilon[:, :], EPS).then_inc(ones_set, 1)
            nc.gpsimd.memset(lt[:, :, :, SPLIT_ROWS:LROWS], 1.0).then_inc(ones_set, 1)
            nc.gpsimd.memset(alt[:, SPLIT_ROWS:LROWS], 1.0).then_inc(ones_set, 1)
            nc.gpsimd.memset(v_all[:, :, :, HD:VW], 1.0).then_inc(ones_set, 1)
            pool.wait_ge(ones_set, 6)
            nc.gpsimd.memset(kt[64:MAX_ROW, :, :].bitcast(F32), 0.0).then_inc(cleared, 1)
            nc.gpsimd.memset(qt[64:MAX_ROW, :, :].bitcast(F32), 0.0).then_inc(cleared, 1)
            pool.wait_ge(cleared, 2)

            pool.wait_ge(mv_ready, B)
            nc.gpsimd.tensor_scalar(ve[:, :], mv[:, :, 1], EPS, None, ALU.add).then_inc(ve_ready, 1)
            pool.wait_ge(ve_ready, 1)
            pool.wait_ge(ones_set, 6)
            nc.gpsimd.tensor_tensor(rs[:, :], ve[:, :], mhalf[:, :], ALU.pow).then_inc(rs_ready, 1)

            def left_parts(ph, g, p):
                step = left_step[ph]
                shift, scale = 2 * ph * LEFT, (2 * ph + 1) * LEFT
                sh = bl[:, bass.ds(g * GB, GB), shift:shift + LEFT]
                L = lt[:, p, :, 0:SPLIT_ROWS].rearrange("p b (r w) -> p b r w", w=LEFT)
                a1 = L[:, :, 0]

                def times(v, r):
                    return v[:, :, None, :].to_broadcast([P, GB, r, LEFT])

                pool.wait_ge(xn_ready[ph], g + 1)
                nc.gpsimd.tensor_tensor(lm[:, :, :], xn[:, p, :, P:D], bl[:, bass.ds(g * GB, GB), scale:scale + LEFT],
                                        ALU.mult).then_inc(step, 1)
                pool.wait_ge(step, 4 * g + 1)
                nc.gpsimd.tensor_tensor(lv[:, :, :], lm[:, :, :], sh, ALU.add).then_inc(step, 1)
                nc.gpsimd.tensor_tensor(L[:, :, 0:3], times(lm, 3), times(sh, 3), ALU.add).then_inc(step, 1)
                pool.wait_ge(step, 4 * g + 3)
                nc.gpsimd.tensor_tensor(lr[:, :, :], lv[:, :, :], a1, ALU.subtract).then_inc(step, 1)
                nc.gpsimd.tensor_tensor(L[:, :, 3:5], times(lv, 2), times(a1, 2), ALU.subtract).then_inc(left_ready[ph], 1)
                pool.wait_ge(step, 4 * g + 4)
                pool.wait_ge(left_ready[ph], 2 * g + 1)
                nc.gpsimd.tensor_tensor(L[:, :, 5], lr[:, :, :], L[:, :, 3], ALU.subtract).then_inc(left_ready[ph], 1)

            pool.wait_ge(bl_in, 16)
            left_parts(0, 0, 0)
            left_parts(0, 1, 1)

            def pool_phase0(g, p):
                pool.wait_ge(xt_done[0], g + 1)
                left_parts(0, g + 2, p)

            with pool.Fori(0, GROUPS // 2 - 1) as i:
                for p in range(2):
                    pool_phase0(2 * i + p, p)

            def alt_parts(v, n):
                pool.wait_ge(at_ready, n + 1 + SPARE)
                pool.wait_ge(att_done, 2 * n + SPARE)
                la = alt[:, 0:SPLIT_ROWS].rearrange("p (r w) -> p r w", w=LEFT)
                nc.gpsimd.tensor_tensor(la[:, 0:3], v[:, None, :].to_broadcast([P, 3, LEFT]),
                                        zeros[:, None, :].to_broadcast([P, 3, LEFT]), ALU.add).then_inc(alt_step, 1)
                pool.wait_ge(alt_step, 2 * n + 1)
                nc.gpsimd.tensor_tensor(alr[:, :], v, la[:, 0], ALU.subtract).then_inc(alt_step, 1)
                nc.gpsimd.tensor_tensor(la[:, 3:5], v[:, None, :].to_broadcast([P, 2, LEFT]),
                                        la[:, 0:1].to_broadcast([P, 2, LEFT]), ALU.subtract).then_inc(alt_ready, 1)
                pool.wait_ge(alt_step, 2 * n + 2)
                pool.wait_ge(alt_ready, 2 * n + 1)
                nc.gpsimd.tensor_tensor(la[:, 5], alr[:, :], la[:, 3], ALU.subtract).then_inc(alt_ready, 1)

            def residual(n):
                pool.wait_ge(pr_ready, n + 1 + SPARE)
                nc.gpsimd.tensor_tensor(x1[:, bass.ds(n, 1)].rearrange("p o d -> p (o d)"), pr[:, :],
                                        xs[:, bass.ds(n, 1)].rearrange("p o d -> p (o d)"), ALU.add).then_inc(x1_ready, 1)

            def pool_attention(u, k, it):
                if isinstance(u, int) and u == 0:
                    return
                alt_parts(at[:, P:D], u - 1)
                residual(u - 1)

            units(pool, pool_attention)
            alt_parts(at[:, P:D], B - 1)
            residual(B - 1)

            def rstd2(g, p):
                pool.wait_ge(mv2_ready, GB * (g + 1))
                nc.gpsimd.tensor_tensor(ve2[:, p], mv2[:, p, :, 1], epsilon[:, :], ALU.add).then_inc(ve2_ready, 1)
                pool.wait_ge(ve2_ready, g + 1)
                nc.gpsimd.tensor_tensor(rs2[:, p], ve2[:, p], mhalf[:, 0:GB], ALU.pow).then_inc(rs2_ready, 1)

            def residual2(it, p):
                g = 2 * it + p
                for b in range(GB):
                    pool.wait_ge(fr_ready, GB * g + b + 1 + SPARE)
                    pool.wait_ge(y_out[p], 16 * it + SPARE)
                    nc.gpsimd.tensor_tensor(yo[:, p, b], fr[:, p, b],
                                            x1[:, bass.ds(g * GB + b, 1)].rearrange("p o d -> p (o d)"),
                                            ALU.add).then_inc(y_ready, 1)

            for g in range(2):
                rstd2(g, g)
                left_parts(1, g, g)
            with pool.Fori(0, GROUPS // 2 - 1) as i:
                for p in range(2):
                    g = 2 * i + p
                    rstd2(g + 2, p)
                    pool.wait_ge(xt_done[1], g + 1)
                    left_parts(1, g + 2, p)
                    residual2(i, p)
            for p in range(2):
                residual2(GROUPS // 2 - 1, p)

        @block.scalar
        def _(act):
            for s in (v_copied, ex_ready, ot_copied, att_copied, g_ready):
                act.sem_inc(s, SPARE)
            act.wait_ge(cond_in, 16)
            nc.scalar.activation(ce[:, :], cs[:, :], ACT.Exp, scale=-1.0).then_inc(silu_exp, 1)
            act.wait_ge(ada_done, 1)
            for q in range(4):
                nc.scalar.activation(mod[:, q, :], bank[2][:, q * B:(q + 1) * B], ACT.Copy, bias=float(q % 2))\
                    .then_inc(mod_ready, 1)

            def modulate(ph, g, p):
                act.wait_ge(xt_done[ph], g + 1)
                for b in range(GB):
                    s = bass.ds(g * GB + b, 1)
                    ins = nc.scalar.activation(ht[:, p, b * N:(b + 1) * N], bank[0][:, b * N:(b + 1) * N], ACT.Identity,
                                               bias=mod[:, 2 * ph, s], scale=mod[:, 2 * ph + 1, s])
                    ins.then_inc(ht_ready[ph], 1)

            act.wait_ge(mod_ready, 4)
            modulate(0, 0, 0)

            def act_phase0(it, p, last):
                g = 2 * it + p
                if not last:
                    modulate(0, g + 1, 1 - p)
                act.wait_ge(parts_out[p], 64 * it + SPARE)
                for c in range(QKC):
                    act.wait_ge(qk_done, QKC * g + c + 1)
                    nc.scalar.activation(qkp[:, p, 0, c, :], bank[2 + c][0:QKR, 0:GT], ACT.Copy).then_inc(hi_ready, 1)
                act.wait_ge(v_done, g + 1)
                nc.scalar.activation(v_all[:, bass.ds(g * GB, GB), :, 0:HD].rearrange("p b h d -> p (b h) d"),
                                     bank[5][:, 0:GB * D].rearrange("p (k d) -> p k d", d=HD),
                                     ACT.Copy).then_inc(v_copied, 1)
                for c in range(QKC):
                    act.wait_ge(rest_ready, QKC * g + c + 1 + SPARE)
                    nc.scalar.activation(qkp[:, p, 1, c, :], qkr[:, p, c, :], ACT.Copy).then_inc(mid_ready, 1)

            with act.Fori(0, GROUPS // 2 - 1) as i:
                for p in range(2):
                    act_phase0(i, p, False)
            act_phase0(GROUPS // 2 - 1, 0, False)
            act_phase0(GROUPS // 2 - 1, 1, True)

            def nmt_copy(b):
                act.wait_ge(nmt_done, b + 1)
                nc.scalar.activation(nmt[:, :], bank[6][0:PARTS * H, 2 * N:2 * N + N // 2].bitcast(BF16), ACT.Copy)\
                    .then_inc(nmt_copied, 1)

            nmt_copy(0)

            def att_copy(n):
                act.wait_ge(att_done, 2 * n + 1 + SPARE)
                act.wait_ge(proj_done, n + SPARE)
                nc.scalar.activation(att[:, :], bank[6][:, 0:N], ACT.Copy).then_inc(att_copied, 1)
                act.wait_ge(att_done, 2 * (n + 1) + SPARE)
                nc.scalar.activation(atl[:, :], bank[7][0:LROWS, 2 * N:2 * N + N // 2].bitcast(BF16), ACT.Copy)\
                    .then_inc(att_copied, 1)

            def act_attention(u, k, it):
                for i in range(QUADS):
                    act.wait_ge(st_done, QUADS * u + i + 1 + SPARE)
                    act.wait_ge(pv_done, QUADS * (u - 1) + i + 1 + SPARE)
                    nc.scalar.activation(ex[:, i, :], bank[2 + i % 2][:, :], ACT.Exp, scale=SCALE).then_inc(ex_ready, 1)
                    if i == 1 and ahead(u, 1):
                        act.wait_ge(max_in, 16 * (u + 1))
                        nmt_copy(u + 1)
                if not (isinstance(u, int) and u == 0):
                    att_copy(u - 1)
                act.wait_ge(pv_done, QUADS * (u + 1) + SPARE)
                act.wait_ge(on_done, u + SPARE)
                nc.scalar.activation(ot[:, :], bank[4][:, :], ACT.Copy).then_inc(ot_copied, 1)

            units(act, act_attention)
            att_copy(B - 1)

            modulate(1, 0, 0)

            def act_mlp(g, p, last):
                for c, (_, m) in enumerate(HCH):
                    act.wait_ge(f1_done, NCH * g + c + 1)
                    act.wait_ge(f2_done, GB * (g - 1) + SPARE)
                    nc.scalar.activation(hg[0:m, p, c, :], bank[2 + c % 4][0:m, 0:GT], ACT.Gelu_apprx_tanh)\
                        .then_inc(g_ready, 1)
                    if c == 2 and not last:
                        modulate(1, g + 1, 1 - p)

            with act.Fori(0, GROUPS // 2 - 1) as i:
                for p in range(2):
                    act_mlp(2 * i + p, p, False)
            act_mlp(GROUPS - 2, 0, False)
            act_mlp(GROUPS - 1, 1, True)

        @block.vector
        def _(dve):
            for s in (lo_ready, rest_ready, pr_ready, at_ready, fr_ready):
                dve.sem_inc(s, SPARE)
            nc.vector.memset(bank[4][:, :], 0.0).then_inc(set_by_dve, 1)
            nc.vector.memset(ctl[:, :], 1.0).then_inc(silu_step, 1)
            nc.vector.memset(hg[96:97, :, NCH - 1, :], 1.0).then_inc(set_by_dve, 1)
            nc.vector.memset(kt[MAX_ROW:SROWS, :, :].bitcast(F32), BF16_ONES).then_inc(set_by_dve, 1)
            dve.wait_ge(silu_exp, 1)
            nc.vector.tensor_scalar(cr[:, :], ce[:, :], 1.0, None, ALU.add).then_inc(silu_step, 1)
            dve.wait_ge(silu_step, 2)
            nc.vector.reciprocal(ce[:, :], cr[:, :]).then_inc(silu_step, 1)
            dve.wait_ge(silu_step, 3)
            nc.vector.tensor_tensor(cr[:, :], cs[:, :], ce[:, :], ALU.mult).then_inc(silu_ready, 1)
            dve.wait_ge(ct_turned, 1)
            nc.vector.tensor_copy(ct[:, :], bank[0][:, 0:B]).then_inc(ct_copied, 1)
            nc.vector.tensor_copy(ctl[0:LEFT, :], bank[0][0:LEFT, B:2 * B]).then_inc(ct_copied, 1)
            dve.wait_ge(ada_done, 2)
            for f in range(2):
                src = bank[6 + f]
                left = 2 * f * LEFT
                nc.vector.tensor_copy(left_r[:, left:left + LEFT], src[0:B, P:D]).then_inc(rows_ready, 1)
                nc.vector.tensor_scalar(left_r[:, left + LEFT:left + 2 * LEFT], src[0:B, D + P:2 * D], 1.0, None,
                                        ALU.add).then_inc(rows_ready, 1)
                nc.vector.tensor_copy(gate_r[:, f * D:(f + 1) * D], src[0:B, 2 * D:3 * D]).then_inc(rows_ready, 1)
            for b in range(B):
                if b % 4 == 0:
                    dve.wait_ge(x_in, 64)
                nc.vector.bn_stats(st[:, b, :], xs[:, b, :]).then_inc(stat_step, 1)
            for b in range(B):
                dve.wait_ge(stat_step, b + 1)
                nc.vector.bn_aggr(mv[:, b, :], st[:, b, :]).then_inc(mv_ready, 1)

            def weight_parts(n, lo, hi):
                c = slice(lo, hi)
                nc.vector.tensor_copy(wlb[:, c], wlf[:, c]).then_inc(wl_step, 1)
                dve.wait_ge(wl_step, 3 * n + 1)
                nc.vector.scalar_tensor_tensor(out=wlr[:, c], in0=wlb[:, c], scalar=msk[:, 0:1], in1=wlf[:, c],
                                               op0=ALU.mult, op1=ALU.add).then_inc(wl_step, 1)
                dve.wait_ge(wl_step, 3 * n + 2)
                nc.vector.tensor_copy(wlb[:, c], wlr[:, c]).then_inc(wl_step, 1)
                dve.wait_ge(wl_step, 3 * n + 3)
                nc.vector.scalar_tensor_tensor(out=wl[:, c], in0=wlb[:, c], scalar=msk[:, 1:2], in1=wlr[:, c],
                                               op0=ALU.mult, op1=ALU.add).then_inc(wl_ready, 1)

            def normalise(ph, g, p):
                for b in range(GB):
                    s = bass.ds(g * GB + b, 1)
                    src = (xs, x1)[ph][:, s].rearrange("p o d -> p (o d)")
                    mean = mv[:, s, 0] if ph == 0 else mv2[:, p, b, 0:1]
                    rstd = rs[:, s] if ph == 0 else rs2[:, p, b:b + 1]
                    ins = nc.vector.tensor_scalar(xn[:, p, b, :], src, mean, rstd, ALU.subtract, ALU.mult)
                ins.then_inc(xn_ready[ph], 1)

            def left_copy(ph, g, p):
                dve.wait_ge(xt_done[ph], g + 1)
                nc.vector.tensor_copy(hl[:, p, :], bank[1][0:LROWS, 0:GT // 2].bitcast(BF16)).then_inc(hl_ready[ph], 1)

            dve.wait_ge(rs_ready, 1)
            normalise(0, 0, 0)
            normalise(0, 1, 1)
            dve.wait_ge(wl_in, 48)
            weight_parts(0, 0, C_P)
            weight_parts(1, C_P, WCOLS)
            left_copy(0, 0, 0)

            def dve_phase0(g, p, more, last):
                if more:
                    dve.wait_ge(xt_done[0], g + 1)
                    normalise(0, g + 2, p)
                if not last:
                    left_copy(0, g + 1, 1 - p)
                dve.wait_ge(lo_ready, QKC * (g - 1) + SPARE)
                for c in range(QKC):
                    dve.wait_ge(hi_ready, QKC * g + c + 1)
                    nc.vector.tensor_tensor(qkr[:, p, c, :], bank[2 + c][0:QKR, 0:GT], qkp[:, p, 0, c, :],
                                            ALU.subtract).then_inc(rest_ready, 1)
                for c in range(QKC):
                    dve.wait_ge(mid_ready, QKC * g + c + 1)
                    nc.vector.tensor_tensor(qkp[:, p, 2, c, :], qkr[:, p, c, :], qkp[:, p, 1, c, :],
                                            ALU.subtract).then_inc(lo_ready, 1)

            with dve.Fori(0, GROUPS // 2 - 1) as i:
                for p in range(2):
                    dve_phase0(2 * i + p, p, True, False)
            dve_phase0(GROUPS - 2, 0, False, False)
            dve_phase0(GROUPS - 1, 1, False, True)

            def negated_max(b, q, i):
                dve.wait_ge(s_done, QUADS * b + i + 1)
                nc.vector.tensor_reduce(nm[:, q, 4 * i:4 * i + 4], bank[i % 2][:, :].rearrange("p (h m) -> p h m", h=4),
                                        AX.X, ALU.max, negate=True).then_inc(max_ready, 1)

            def max_parts(b, q):
                dve.wait_ge(max_ready, QUADS * (b + 1))
                dve.wait_ge(nmt_done, b)
                nc.vector.tensor_copy(nmp[:, 0, :], nm[:, q, :]).then_inc(nm_step, 1)
                dve.wait_ge(nm_step, 3 * b + 1)
                nc.vector.tensor_tensor(nmr[:, :], nm[:, q, :], nmp[:, 0, :], ALU.subtract).then_inc(nm_step, 1)
                nc.vector.tensor_tensor(nmp[:, 1, :], nm[:, q, :], nmp[:, 0, :], ALU.subtract).then_inc(nm_step, 1)
                dve.wait_ge(nm_step, 3 * b + 3)
                nc.vector.tensor_tensor(nmp[:, 2, :], nmr[:, :], nmp[:, 1, :], ALU.subtract).then_inc(nm_ready, 1)

            for i in range(QUADS):
                negated_max(0, 0, i)
            max_parts(0, 0)
            for i in range(QUADS):
                negated_max(1, 1, i)
            max_parts(1, 1)

            heads = bank[5][:, :].rearrange("p (h w) -> p h w", h=H)

            def dve_denominators(n):
                dve.wait_ge(on_done, n + 1 + SPARE)
                nc.vector.reciprocal(rd[:, :], heads[:, :, HD]).then_inc(rd_ready, 1)

            def dve_divide(n):
                dve.wait_ge(rd_ready, n + 1)
                dve.wait_ge(att_done, 2 * n + SPARE)
                nc.vector.tensor_tensor(at[:, :].rearrange("p (h d) -> p h d", h=H), heads[:, :, 0:HD],
                                        rd[:, :, None].to_broadcast([P, H, HD]), ALU.mult).then_inc(at_ready, 1)

            def gate(n):
                dve.wait_ge(proj_done, n + 1 + SPARE)
                dve.wait_ge(x1_ready, n + SPARE)
                nc.vector.tensor_tensor(pr[:, :], bank[7][:, 0:D], gates[:, bass.ds(n, 1), 0:D].rearrange("p o d -> p (o d)"),
                                        ALU.mult).then_inc(pr_ready, 1)

            dve.wait_ge(gates_in, 16)

            def dve_attention(u, k, it):
                tail = not (isinstance(u, int) and u == 0)
                if tail:
                    dve_denominators(u - 1)
                    dve_divide(u - 1)
                if ahead(u, 2):
                    for i in range(QUADS):
                        negated_max(u + 2, k % 2, i)
                    max_parts(u + 2, k % 2)
                if tail:
                    gate(u - 1)

            units(dve, dve_attention)
            dve_denominators(B - 1)
            dve_divide(B - 1)
            gate(B - 1)

            def statistics2(g, p):
                for b in range(GB):
                    dve.wait_ge(x1_ready, GB * g + b + 1 + SPARE)
                    nc.vector.bn_stats(st2[:, p, b, :], x1[:, bass.ds(g * GB + b, 1)].rearrange("p o d -> p (o d)"))\
                        .then_inc(st2_done, 1)
                dve.wait_ge(st2_done, GB * (g + 1))
                dve.sem_inc(passed, 1)
                for b in range(GB):
                    nc.vector.bn_aggr(mv2[:, p, b, :], st2[:, p, b, :]).then_inc(mv2_ready, 1)

            def gate2(g, p):
                for b in range(GB):
                    dve.wait_ge(f2_done, GB * g + b + 1 + SPARE)
                    dve.wait_ge(y_ready, GB * (g - 1) + SPARE)
                    nc.vector.tensor_tensor(fr[:, p, b, :], bank[6 + b][:, 0:D],
                                            gates[:, bass.ds(g * GB + b, 1), D:2 * D].rearrange("p o d -> p (o d)"),
                                            ALU.mult).then_inc(fr_ready, 1)

            for g in range(2):
                statistics2(g, g)
            for g in range(2):
                dve.wait_ge(rs2_ready, g + 1)
                normalise(1, g, g)
            left_copy(1, 0, 0)

            def dve_mlp(g, p, more, last):
                if more:
                    statistics2(g + 2, p)
                    dve.wait_ge(rs2_ready, g + 3)
                    dve.wait_ge(xt_done[1], g + 1)
                    normalise(1, g + 2, p)
                if not last:
                    left_copy(1, g + 1, 1 - p)
                gate2(g, p)

            with dve.Fori(0, GROUPS // 2 - 1) as i:
                for p in range(2):
                    dve_mlp(2 * i + p, p, True, False)
            dve_mlp(GROUPS - 2, 0, False, False)
            dve_mlp(GROUPS - 1, 1, False, True)

        @block.tensor
        def _(pe):
            for s in (pv_done, st_done, on_done, att_done, proj_done, f2_done):
                pe.sem_inc(s, SPARE)
            pe.wait_ge(consts, 2)
            pe.wait_ge(silu_ready, 1)
            nc.tensor.transpose(bank[0][:, 0:B], cr[:, 0:P], ident[0:B, 0:B])
            nc.tensor.transpose(bank[0][0:LEFT, B:2 * B], cr[:, P:D], ident[0:B, 0:B]).then_inc(ct_turned, 1)
            pe.wait_ge(ct_copied, 2)
            pe.wait_ge(wa_in, 32)
            for n, q in enumerate((0, 1, 3, 4)):
                dst = bank[2][:, n * B:(n + 1) * B]
                nc.tensor.matmul(dst, wa[:, q * D:q * D + P], ct[:, :], start=True, stop=False)
                mm = nc.tensor.matmul(dst, wal[:, q * D:q * D + P], ctl[:, :], start=False, stop=True)
            mm.then_inc(ada_done, 1)
            for f in range(2):
                dst, c = bank[6 + f][0:B, 0:3 * D], slice(f * 3 * D, (f + 1) * 3 * D)
                nc.tensor.matmul(dst, ct[:, :], wa[:, c], start=True, stop=False)
                mm = nc.tensor.matmul(dst, ctl[:, :], wal[:, c], start=False, stop=True)
            mm.then_inc(ada_done, 1)

            def turn(ph, g, p):
                pe.wait_ge(xn_ready[ph], g + 1)
                for b in range(GB):
                    nc.tensor.transpose(bank[0][:, b * N:(b + 1) * N], xn[:, p, b, 0:P], ident[:, :])
                pe.wait_ge(left_ready[ph], 2 * (g + 1))
                parts = bank[1][0:LROWS, 0:GT // 2].bitcast(BF16)
                for b in range(GB):
                    mm = nc.tensor.transpose(parts[:, b * N:(b + 1) * N], lt[:, p, b, :], ident_b[:, :])
                mm.then_inc(xt_done[ph], 1)

            pe.wait_ge(ones_set, 6)
            turn(0, 0, 0)
            pe.wait_ge(wm_in, 16)
            pe.wait_ge(wl_ready, 2)
            pe.wait_ge(mod_ready, 4)
            pe.wait_ge(cleared, 2)
            pe.wait_ge(set_by_dve, 3)

            def pe_phase0(g, p, last):
                if not last:
                    pe.wait_ge(ht_ready[0], GB * (g + 1))
                    pe.wait_ge(hl_ready[0], g + 1)
                    turn(0, g + 1, 1 - p)
                else:
                    pe.wait_ge(ht_ready[0], GB * (g + 1))
                    pe.wait_ge(hl_ready[0], g + 1)
                for c in range(QKC):
                    pe.wait_ge(rest_ready, QKC * (g - 1) + c + 1 + SPARE)
                    w = slice(c * QKR, (c + 1) * QKR)
                    dst = bank[2 + c][0:QKR, 0:GT]
                    nc.tensor.matmul(dst, wm[:, w], ht[:, p, :], start=True, stop=False)
                    nc.tensor.matmul(dst, wl[:, w], hl[:, p, :], start=False, stop=True).then_inc(qk_done, 1)
                pe.wait_ge(v_copied, g + SPARE)
                for b in range(GB):
                    dst, t = bank[5][:, b * D:(b + 1) * D], slice(b * N, (b + 1) * N)
                    nc.tensor.matmul(dst, ht[:, p, t], wm[:, C_V:C_P], start=True, stop=False)
                    mm = nc.tensor.matmul(dst, hl[:, p, t], wl[:, C_V:C_P], start=False, stop=True)
                mm.then_inc(v_done, 1)

            with pe.Fori(0, GROUPS // 2 - 1) as i:
                for p in range(2):
                    pe_phase0(2 * i + p, p, False)
            pe_phase0(GROUPS - 2, 0, False)
            pe_phase0(GROUPS - 1, 1, True)

            def scores_q(b, slot, i):
                for j in range(4):
                    mm = nc.tensor.matmul(bank[i % 2][:, j * N:(j + 1) * N], qt[0:MAX_ROW, slot, head(i, j)],
                                          kt[0:MAX_ROW, slot, head(i, j)], start=True, stop=True)
                mm.then_inc(s_done, 1)

            def scores_k(slot, i):
                for j in range(4):
                    mm = nc.tensor.matmul(bank[2 + i % 2][:, j * N:(j + 1) * N], kt[0:SROWS, slot, head(i, j)],
                                          qt[0:SROWS, slot, head(i, j)], start=True, stop=True)
                mm.then_inc(st_done, 1)

            def values(slot, i):
                for j in range(4):
                    mm = nc.tensor.matmul(bank[4][32 * j:32 * j + VW, i * N:(i + 1) * N], vt[:, slot, 4 * i + j, :],
                                          ex[:, i, j * N:(j + 1) * N], start=True, stop=True)
                mm.then_inc(pv_done, 1)

            def turn_max():
                pe.sem_inc(passed, 1)
                nc.tensor.transpose(bank[6][0:PARTS * H, 2 * N:2 * N + N // 2].bitcast(BF16),
                                    nmp[:, :, :].rearrange("p l h -> p (l h)"), ident_b[:, :]).then_inc(nmt_done, 1)

            pe.wait_ge(cleared, 2)
            pe.wait_ge(set_by_dve, 3)
            for b in range(2):
                pe.wait_ge(qk_in[b], 32)
                for i in range(QUADS):
                    if b + i // 2 > 0:
                        pe.wait_ge(max_ready, QUADS * b + i - 1)
                    scores_q(b, b, i)
                if b == 0:
                    pe.wait_ge(nm_ready, 1)
                    turn_max()
            pe.wait_ge(rest_ready, QKC * GROUPS + SPARE)
            pe.wait_ge(v_copied, GROUPS + SPARE)

            def turn_result(n):
                pe.wait_ge(ot_copied, n + 1 + SPARE)
                pe.wait_ge(at_ready, n + SPARE)
                for i in range(QUADS):
                    mm = nc.tensor.transpose(bank[5][:, i * N:(i + 1) * N], ot[:, i * N:(i + 1) * N], ident[:, :])
                mm.then_inc(on_done, 1)

            def turn_back(n):
                pe.wait_ge(at_ready, n + 1 + SPARE)
                nc.tensor.transpose(bank[6][:, 0:N], at[:, 0:P], ident[:, :]).then_inc(att_done, 1)

            def turn_back_parts(n):
                pe.wait_ge(alt_ready, 2 * (n + 1))
                pe.wait_ge(pr_ready, n + SPARE)
                nc.tensor.transpose(bank[7][0:LROWS, 2 * N:2 * N + N // 2].bitcast(BF16), alt[:, :], ident_b[:, :])\
                    .then_inc(att_done, 1)

            def project(n):
                pe.wait_ge(att_copied, 2 * (n + 1) + SPARE)
                nc.tensor.matmul(bank[7][:, 0:D], att[:, :], wm[:, C_P:C_F], start=True, stop=False)
                nc.tensor.matmul(bank[7][:, 0:D], atl[:, :], wl[:, C_P:C_F], start=False, stop=True).then_inc(proj_done, 1)

            def pe_attention(u, k, it):
                tail = not (isinstance(u, int) and u == 0)
                k2 = (k + 2) % SLOTS

                def keys(i):
                    pe.wait_ge(ex_ready, QUADS * u + i - 1 + SPARE)
                    scores_k(k % SLOTS, i)

                def pv(i):
                    pe.wait_ge(ex_ready, QUADS * u + i + 1 + SPARE)
                    values(k % SLOTS, i)

                def queries(i):
                    if ahead(u, 2):
                        pe.wait_ge(max_ready, QUADS * (u + 2) + i - 1)
                        scores_q(u + 2, k2, i)

                pe.wait_ge(max_in, 16 * (u + 1))
                keys(0)
                keys(1)
                if tail:
                    turn_result(u - 1)
                if ahead(u, 1):
                    pe.wait_ge(nm_ready, u + 2)
                    pe.wait_ge(att_copied, 2 * (u - 1) + SPARE)
                    turn_max()
                if ahead(u, 2):
                    pe.wait_ge(qk_in[k2], 32 * (it + 1 + (k + 2) // SLOTS))
                queries(0)
                pe.wait_ge(v_in[k % SLOTS], 16 * (it + 1 + k // SLOTS))
                pe.wait_ge(ot_copied, u + SPARE)
                pv(0)
                keys(2)
                queries(1)
                pv(1)
                keys(3)
                if tail:
                    if ahead(u, 1):
                        pe.wait_ge(nmt_copied, u + 2)
                    turn_back(u - 1)
                queries(2)
                pv(2)
                queries(3)
                if tail:
                    turn_back_parts(u - 1)
                pv(3)
                if tail:
                    project(u - 1)

            pe.wait_ge(wrest_in, 16)
            units(pe, pe_attention)
            turn_result(B - 1)
            turn_back(B - 1)
            turn_back_parts(B - 1)
            project(B - 1)

            turn(1, 0, 0)
            pe.wait_ge(w2_in, 48)
            pe.wait_ge(pr_ready, B + SPARE)

            def pe_mlp(g, p, last):
                def hidden(c):
                    before = NCH * g if c == 0 else NCH * g + 1 if c == 4 else NCH * (g - 1) + c + 1
                    pe.wait_ge(g_ready, before + SPARE)
                    h0, m = HCH[c]
                    w = slice(C_F + h0, C_F + h0 + m)
                    dst = bank[2 + c % 4][0:m, 0:GT]
                    nc.tensor.matmul(dst, wm[:, w], ht[:, p, :], start=True, stop=False)
                    nc.tensor.matmul(dst, wl[:, w], hl[:, p, :], start=False, stop=True).then_inc(f1_done, 1)

                pe.wait_ge(ht_ready[1], GB * (g + 1))
                pe.wait_ge(hl_ready[1], g + 1)
                for c in range(3):
                    hidden(c)
                if not last:
                    turn(1, g + 1, 1 - p)
                hidden(3)
                hidden(4)
                for b in range(GB):
                    pe.wait_ge(fr_ready, GB * (g - 1) + b + 1 + SPARE)
                    for c, (_, m) in enumerate(HCH):
                        rows = m + (c == NCH - 1)
                        if b == 0:
                            pe.wait_ge(g_ready, NCH * g + c + 1 + SPARE)
                        mm = nc.tensor.matmul(bank[6 + b][:, 0:D], hg[0:rows, p, c, b * N:(b + 1) * N],
                                              w2[0:rows, c, :], start=(c == 0), stop=(c == NCH - 1))
                    mm.then_inc(f2_done, 1)

            with pe.Fori(0, GROUPS // 2 - 1) as i:
                for p in range(2):
                    pe_mlp(2 * i + p, p, False)
            pe_mlp(GROUPS - 2, 0, False)
            pe_mlp(GROUPS - 1, 1, True)


def part_masks():
    part = np.array([n for m in range(PARTS) for n in range(PARTS - m) for _ in range(LEFT)] + list(range(PARTS)))
    return np.stack([-(part > 0).astype(np.float32), -(part > 1).astype(np.float32)], axis=1)


def kernel(x, cond_1152, L0_cond_w_qkv, L0_cond_b_qkv, L0_cond_w_proj, L0_cond_b_proj, L0_cond_w_fc1,
           L0_cond_b_fc1, L0_cond_w_fc2, L0_cond_b_fc2, L0_cond_w_ada, L0_cond_b_ada):
    from concourse import bacc
    from concourse.bass_utils import run_bass_kernel_spmd

    def with_bias(w, b):
        return np.concatenate([np.asarray(w), np.asarray(b)[None]], axis=0)

    qkv = with_bias(L0_cond_w_qkv, L0_cond_b_qkv)
    qk = qkv[:, 0:2 * D].reshape(D + 1, 2, H, QKC, HD // QKC).transpose(0, 3, 4, 1, 2).reshape(D + 1, 2 * D)
    arrays = {
        "x": np.asarray(x),
        "cond": np.asarray(cond_1152),
        "w_all": np.concatenate([qk, qkv[:, 2 * D:], with_bias(L0_cond_w_proj, L0_cond_b_proj),
                                 with_bias(L0_cond_w_fc1, L0_cond_b_fc1)], axis=1),
        "w_fc2": with_bias(L0_cond_w_fc2, L0_cond_b_fc2),
        "w_ada": with_bias(L0_cond_w_ada, L0_cond_b_ada),
        "masks": part_masks(),
    }
    arrays = {f"in_{k}": np.ascontiguousarray(a) for k, a in arrays.items()}
    nc = bacc.Bacc("TRN2", target_bir_lowering=False, num_devices=1)
    args = [nc.dram_tensor(k, a.shape, mybir.dt.from_np(a.dtype), kind="ExternalInput").ap() for k, a in arrays.items()]
    args.append(nc.dram_tensor("out_x", (B, N, D), F32, kind="ExternalOutput").ap())
    build(nc, *args)
    result = run_bass_kernel_spmd(nc, [arrays], core_ids=[0])
    return result.results[0]["out_x"]
```

```python
from contextlib import ExitStack

import numpy as np

import concourse.bass as bass
from concourse import mybir

F32 = mybir.dt.float32
BF16 = mybir.dt.bfloat16
ACT = mybir.ActivationFunctionType
ALU = mybir.AluOpType
AX = mybir.AxisListType

B, N, D, H = 16, 128, 144, 16
HD = D // H
HID = 4 * D
P = 128
EPS = 1e-6
SCALE = float(HD) ** -0.5
LEFT = D - P
PARTS = 3
SPLIT_ROWS = 6 * LEFT
LROWS = SPLIT_ROWS + PARTS
GB = 2
GT = GB * N
GROUPS = B // GB
FIRST = 2 * GB
RING = 3
TURNS = 2
WHOLE = RING * TURNS
QKC = 3
QKR = 2 * D // QKC
PROD_ROWS = PARTS * PARTS * HD
MAX_ROW = 96
SROWS = MAX_ROW + PARTS
QUADS = H // 4
VW = HD + 1
SLOTS = 4
HCH = [(0, 128), (128, 128), (256, 128), (384, 96), (480, 96)]
NCH = len(HCH)
WCOLS = 3 * D + D + HID
C_V, C_P, C_F = 2 * D, 3 * D, 4 * D
BF16_ONES = float(np.array([0x3F803F80], np.uint32).view(np.float32)[0])
SPARE = 128


def build(nc, x, cond, w_all, w_fc2, w_ada, masks, fill, out):
    ctx = ExitStack()
    with ctx:
        def sb(name, shape, dt=F32):
            return ctx.enter_context(nc.sbuf_tensor(name, shape, dt))

        def sem(name):
            return ctx.enter_context(nc.semaphore(name))

        bank = [ctx.enter_context(nc.psum_tensor(f"bank{i}", [P, 512], F32)) for i in range(8)]

        parts_d = nc.dram_tensor("parts_d", [B, PARTS + 2, HD, 2, H, N], BF16, kind="Internal").ap()
        left_d = nc.dram_tensor("left_d", [B, 4 * LEFT], F32, kind="Internal").ap()
        gate_d = nc.dram_tensor("gate_d", [B, 2 * D], F32, kind="Internal").ap()

        ident = sb("ident", [P, P])
        ident_b = sb("ident_b", [P, P], BF16)
        zeros = sb("zeros", [P, H])
        epsilon = sb("epsilon", [P, GB])
        mhalf = sb("mhalf", [P, B])
        msk = sb("msk", [LROWS, 2])
        wm = sb("wm", [P, WCOLS])
        wl = sb("wl", [LROWS, WCOLS], BF16)
        wlf = sb("wlf", [LROWS, WCOLS])
        wlr = sb("wlr", [LROWS, WCOLS])
        wlb = sb("wlb", [LROWS, WCOLS], BF16)
        wlt = sb("wlt", [LROWS, WCOLS - C_P])
        w2 = sb("w2", [P, NCH, D])
        wa = sb("wa", [P, 6 * D])
        wal = sb("wal", [LEFT + 1, 6 * D])
        cs = sb("cs", [B, D])
        ce = sb("ce", [B, D])
        cr = sb("cr", [B, D])
        ct = sb("ct", [P, B])
        ctl = sb("ctl", [LEFT + 1, B])
        mod = sb("mod", [P, 4, B])
        left_r = sb("left_r", [B, 4 * LEFT])
        gate_r = sb("gate_r", [B, 2 * D])
        bl = sb("bl", [P, B, 4 * LEFT])
        gates = sb("gates", [P, B, 2 * D])
        ones = sb("ones", [B, P])
        spread = sb("spread", [B, FIRST, 2 * LEFT])
        bl_first = sb("bl_first", [P, FIRST, 2 * LEFT])
        xs = sb("xs", [P, B, D])
        x1 = sb("x1", [P, B, D])
        st = sb("st", [P, B, 6])
        mv = sb("mv", [P, B, 2])
        ve = sb("ve", [P, B])
        rs = sb("rs", [P, B])
        st2 = sb("st2", [P, 2, GB, 6])
        mv2 = sb("mv2", [P, 2, GB, 2])
        ve2 = sb("ve2", [P, 2, GB])
        rs2 = sb("rs2", [P, 2, GB])
        xn = sb("xn", [P, RING, GB, D])
        lm = sb("lm", [P, GB, LEFT])
        lv = sb("lv", [P, GB, LEFT])
        lr = sb("lr", [P, GB, LEFT])
        lt = sb("lt", [P, RING, GB, LROWS], BF16)
        ht = sb("ht", [P, RING, GT])
        hl = sb("hl", [LROWS, RING, GT], BF16)
        qkp = sb("qkp", [QKR, RING, PARTS, QKC, GT], BF16)
        qkr = sb("qkr", [QKR, RING, QKC, GT])
        v_all = sb("v_all", [P, B, H, VW])
        qt = sb("qt", [P, SLOTS, H * N], BF16)
        kt = sb("kt", [P, SLOTS, H * N], BF16)
        vt = sb("vt", [P, SLOTS, H, VW])
        nm = sb("nm", [P, 2, H])
        nmr = sb("nmr", [P, H])
        nmp = sb("nmp", [P, PARTS, H], BF16)
        nmt = sb("nmt", [PARTS * H, N], BF16)
        ex = sb("ex", [P, QUADS, 4 * N])
        ot = sb("ot", [P, QUADS * N])
        rd = sb("rd", [P, H])
        at = sb("at", [P, D])
        alr = sb("alr", [P, LEFT])
        alt = sb("alt", [P, LROWS], BF16)
        att = sb("att", [P, N])
        atl = sb("atl", [LROWS, N], BF16)
        pr = sb("pr", [P, D])
        hg = sb("hg", [P, 2, NCH, GT])
        fr = sb("fr", [P, 2, GB, D])
        yo = sb("yo", [P, 2, GB, D])

        passed = sem("passed")
        cond_in, wa_in, wm_in, wrest_in, wl_in, wl2_in, w2_in = (sem(n) for n in (
            "cond_in", "wa_in", "wm_in", "wrest_in", "wl_in", "wl2_in", "w2_in"))
        x_in = [sem(f"x_in{q}") for q in range(4)]
        consts, ident_zero, fill_in, set_by_dve = sem("consts"), sem("ident_zero"), sem("fill_in"), sem("set_by_dve")
        silu_exp, silu_step, silu_ready = sem("silu_exp"), sem("silu_step"), sem("silu_ready")
        ct_turned, ct_copied, ada_done, mod_ready = sem("ct_turned"), sem("ct_copied"), sem("ada_done"), sem("mod_ready")
        spread_ready, spread_done, first_ready = sem("spread_ready"), sem("spread_done"), sem("first_ready")
        rows_ready, bl_in = sem("rows_ready"), sem("bl_in")
        gates_in = [sem("gates_in0"), sem("gates_in2")]
        left_out, gate_out = sem("left_out"), sem("gate_out")
        wl_step, wl_ready = sem("wl_step"), sem("wl_ready")
        wl2_step, wl2_ready = sem("wl2_step"), sem("wl2_ready")
        stat_step, mv_ready, ve_ready, rs_ready = sem("stat_step"), sem("mv_ready"), sem("ve_ready"), sem("rs_ready")
        xn_ready = [sem("xn_ready0"), sem("xn_ready2")]
        left_step = [sem("left_step0"), sem("left_step2")]
        left_ready = [sem("left_ready0"), sem("left_ready2")]
        xt_done = [sem("xt_done0"), sem("xt_done2")]
        ht_ready = [sem("ht_ready0"), sem("ht_ready2")]
        hl_ready = [sem("hl_ready0"), sem("hl_ready2")]
        qk_done, hi_ready, rest_ready, mid_ready, lo_ready = (sem(n) for n in (
            "qk_done", "hi_ready", "rest_ready", "mid_ready", "lo_ready"))
        v_done, v_copied, ones_set = sem("v_done"), sem("v_copied"), sem("ones_set")
        parts_out = [sem(f"parts_out{p}") for p in range(RING)]
        last_out = sem("last_out")
        again_out = [sem(f"again_out{p}") for p in range(RING)]
        qk_in, v_in = ([sem(f"{n}{k}") for k in range(SLOTS)] for n in ("qk_in", "v_in"))
        max_in = sem("max_in")
        s_done, max_ready, nm_step, nm_ready = sem("s_done"), sem("max_ready"), sem("nm_step"), sem("nm_ready")
        nmt_done, nmt_copied = sem("nmt_done"), sem("nmt_copied")
        st_done, ex_ready, pv_done, ot_copied = sem("st_done"), sem("ex_ready"), sem("pv_done"), sem("ot_copied")
        on_done, rd_ready, at_ready = sem("on_done"), sem("rd_ready"), sem("at_ready")
        alt_step, alt_ready, att_done, att_copied = sem("alt_step"), sem("alt_ready"), sem("att_done"), sem("att_copied")
        proj_done, pr_ready, x1_ready = sem("proj_done"), sem("pr_ready"), sem("x1_ready")
        st2_done, mv2_ready, ve2_ready, rs2_ready = sem("st2_done"), sem("mv2_ready"), sem("ve2_ready"), sem("rs2_ready")
        f1_done, g_ready, f2_done, fr_ready, y_ready = (sem(n) for n in (
            "f1_done", "g_ready", "f2_done", "fr_ready", "y_ready"))
        last_ready, y_last = sem("last_ready"), [sem(f"y_last{b}") for b in range(GB)]
        y_out = [sem(f"y_out{p}") for p in range(2)]

        block = ctx.enter_context(nc.Block())

        x_tok = x.rearrange("b n d -> n b d")
        out_tok = out.rearrange("b n d -> n b d")

        def head(i, j):
            h = 4 * i + j
            return slice(h * N, (h + 1) * N)

        def again(engine, g, p, n, signal):
            engine.wait_ge(parts_out[p], SPARE + 16 * GB * (n + 1))
            q = parts_d[bass.ds(g * GB, GB), :, :, 0]
            first = q[:, 0:2].rearrange("b l d h t -> (l d) b (h t)")
            behind = q[:, PARTS:PARTS + 2].rearrange("b l d h t -> (l d) b (h t)")
            engine.dma_start(behind, first).then_inc(signal, 16)

        def scored(g):
            return g - WHOLE if isinstance(g, int) and g >= WHOLE else None

        def score_bank(b, i):
            return bank[i % 2 + (6 if isinstance(b, int) and b == 0 else 0)]

        def units(engine, unit):
            unit(0, 0, 0)
            with engine.Fori(0, B // SLOTS - 1) as it:
                for k in range(SLOTS):
                    unit(SLOTS * it + 1 + k, 1 + k, it)
            for k in range(SLOTS - 1):
                unit(B - SLOTS + 1 + k, 1 + k, B // SLOTS - 1)

        def ahead(u, n):
            return not isinstance(u, int) or u + n < B

        @block.sync
        def _(sp):
            for s in (*parts_out, *again_out, *y_out):
                sp.sem_inc(s, SPARE)
            sp.dma_start(cs[:, :], cond).then_inc(cond_in, 16)
            sp.dma_start(wa[:, :], w_ada[0:P, :]).then_inc(wa_in, 16)
            sp.dma_start(wal[:, :], w_ada[P:D + 1, :]).then_inc(wa_in, 16)

            def x_load(q):
                sp.dma_start(xs[:, 4 * q:4 * q + 4, :], x_tok[:, 4 * q:4 * q + 4, :]).then_inc(x_in[q], 16)

            def left_rows_load(lo, hi, sem_in):
                lrows, brow, n = w_all[P:D, lo:hi], w_all[D:D + 1, lo:hi], hi - lo
                sp.dma_start(wlf[0:SPLIT_ROWS, lo:hi], bass.AP(tensor=lrows.tensor, offset=lrows.offset,
                             ap=[[0, 6], [WCOLS, LEFT], [1, n]])).then_inc(sem_in, 16)
                sp.dma_start(wlf[SPLIT_ROWS:LROWS, lo:hi], bass.AP(tensor=brow.tensor, offset=brow.offset,
                             ap=[[0, PARTS], [1, n]])).then_inc(sem_in, 16)

            x_load(0)
            sp.dma_start(msk[:, :], masks).then_inc(wl_in, 16)
            left_rows_load(0, C_P, wl_in)
            sp.dma_start(wm[:, 0:C_P], w_all[0:P, 0:C_P]).then_inc(wm_in, 16)
            x_load(1)
            sp.wait_ge(rows_ready, 2)
            sp.dma_start(left_d, left_r[:, :]).then_inc(left_out, 16)
            sp.wait_ge(left_out, 16)
            sp.dma_start(bl[:, :, :], bass.AP(tensor=left_d.tensor, offset=left_d.offset,
                         ap=[[0, P], [1, B * 4 * LEFT]])).then_inc(bl_in, 16)
            x_load(2)
            x_load(3)
            for tile, rows in ((kt, SROWS - PROD_ROWS), (qt, MAX_ROW - PROD_ROWS)):
                sp.dma_start(tile[PROD_ROWS:PROD_ROWS + rows, :, :].bitcast(F32), bass.AP(tensor=fill.tensor,
                             offset=fill.offset, ap=[[H * N // 2, rows], [0, SLOTS], [1, H * N // 2]])).then_inc(fill_in, 16)
            sp.wait_ge(rows_ready, 3)
            sp.dma_start(gate_d, gate_r[:, :]).then_inc(gate_out, 16)
            left_rows_load(C_P, WCOLS, wl2_in)
            sp.dma_start(wm[:, C_P:WCOLS], w_all[0:P, C_P:WCOLS]).then_inc(wrest_in, 16)
            sp.wait_ge(gate_out, 16)

            def gate_load(f):
                src = gate_d[:, f * D:(f + 1) * D]
                sp.dma_start(gates[:, :, f * D:(f + 1) * D], bass.AP(tensor=src.tensor, offset=src.offset,
                             ap=[[0, P], [2 * D, B], [1, D]])).then_inc(gates_in[f], 16)

            gate_load(0)

            def parts_store(g, p):
                sp.wait_ge(lo_ready, QKC * (g + 1) + SPARE)
                for b in range(GB):
                    dst = parts_d[bass.ds(g * GB + b, 1), 0:PARTS].rearrange("o l (c e) a h t -> (e a h) (o l c) t", c=QKC)
                    src = qkp[:, p, :, :, b * N:(b + 1) * N].rearrange("p l c t -> p (l c) t")
                    sp.dma_start(dst, src).then_inc(parts_out[p], 16)

            def qk_load(b, slot):
                k = parts_d[bass.ds(b, 1), 0:PARTS, :, 1].rearrange("o l d h t -> (o l d) (h t)")
                q = parts_d[bass.ds(b, 1), 0:PARTS, :, 0].rearrange("o l d h t -> (o l d) (h t)")
                row, block_of = 2 * H * N, HD * 2 * H * N
                for tile, a, rot in ((kt, k, 0), (qt, q, block_of)):
                    src = bass.AP(tensor=a.tensor, offset=a.offset, ap=[[row, PARTS * HD], [rot, PARTS], [1, H * N]])
                    sp.dma_start(tile[0:PROD_ROWS, slot, :], src).then_inc(qk_in[slot], 16)

            def v_load(b, slot):
                sp.dma_start(vt[:, slot], v_all[:, bass.ds(b, 1)].rearrange("p o h w -> p (o h) w")).then_inc(v_in[slot], 16)

            def max_load(b, slot):
                sp.wait_ge(nmt_copied, b + 1)
                sp.dma_start(qt[MAX_ROW:SROWS, slot, :], nmt[:, :]).then_inc(max_in, 16)

            def group(g):
                parts_store(g, g % RING)
                if g > 0:
                    p, n = (g - 1) % RING, (g - 1) // RING
                    sp.wait_ge(again_out[p], SPARE + 16 * n)
                    again(sp, g - 1, p, n, again_out[p])

            sp.wait_ge(fill_in, 32)
            for g in range(WHOLE + 1):
                if g == WHOLE:
                    max_load(0, 0)
                    sp.wait_ge(v_copied, SPARE + 1)
                    for b in range(2):
                        v_load(b, b)
                group(g)
                for b in range(3):
                    if g == (2, 4, 5)[b]:
                        sp.wait_ge(again_out[b // GB], SPARE + 16)
                        qk_load(b, b)
            qk_load(3, 3)
            max_load(1, 1)
            group(WHOLE + 1)

            def attention_loads(u, k, it):
                if k == 3:
                    for p, n in ((0, TURNS + 1), (1, TURNS), (2, TURNS)):
                        sp.wait_ge(again_out[p], SPARE + 16 * n)
                    sp.wait_ge(last_out, 16)
                begun = isinstance(u, int) and u == 0
                if ahead(u, 3) and not begun:
                    sp.wait_ge(st_done, 4 * u + SPARE)
                    sp.sem_inc(passed, 1)
                    qk_load(u + 3, (k + 3) % SLOTS)
                if ahead(u, 1) and not begun:
                    max_load(u + 1, (k + 1) % SLOTS)
                if isinstance(u, int) and u == B - 3:
                    sp.dma_start(w2[:, 0:3, :], w_fc2[0:3 * P, :].rearrange("(c p) n -> p c n", p=P)).then_inc(w2_in, 16)
                    sp.dma_start(w2[0:96, 3, :], w_fc2[HCH[3][0]:HCH[4][0], :]).then_inc(w2_in, 16)
                    sp.dma_start(w2[0:97, 4, :], w_fc2[HCH[4][0]:HID + 1, :]).then_inc(w2_in, 16)
                    gate_load(1)
                if ahead(u, 2):
                    sp.wait_ge(pv_done, 4 * (u - 1) + SPARE)
                    sp.sem_inc(passed, 1)
                    v_load(u + 2, (k + 2) % SLOTS)
                if isinstance(u, int) and u == 0:
                    sp.wait_ge(again_out[2], SPARE + 16 * TURNS)
                    sp.wait_ge(v_copied, SPARE + GROUPS)

            units(sp, attention_loads)

            def store(g, p):
                sp.wait_ge(y_ready, GB * (g + 1) + SPARE)
                sp.dma_start(out_tok[:, bass.ds(g * GB, GB), :], yo[:, p]).then_inc(y_out[p], 16)

            with sp.Fori(0, GROUPS // 2 - 1) as i:
                for p in range(2):
                    store(2 * i + p, p)
            store(GROUPS - 2, 0)
            for b in range(GB):
                sp.wait_ge(last_ready, b + 1)
                sp.dma_start(out_tok[:, B - GB + b, :], yo[:, 1, b]).then_inc(y_last[b], 16)
                sp.wait_ge(y_out[b], SPARE + 16 * (GROUPS // 2 - b))
            for b in range(GB):
                sp.wait_ge(y_last[b], 16)

        @block.gpsimd
        def _(pool):
            for s in (x1_ready, y_ready):
                pool.sem_inc(s, SPARE)
            nc.gpsimd.memset(ident[:, :], 0.0).then_inc(ident_zero, 1)
            nc.gpsimd.memset(ident_b[:, :], 0.0).then_inc(ident_zero, 1)
            pool.wait_ge(ident_zero, 2)
            for m in (ident, ident_b):
                nc.gpsimd.affine_select(out=m[:, :], in_=m[:, :], compare_op=ALU.not_equal, fill=1.0, base=0,
                                        pattern=[[-1, P]], channel_multiplier=1).then_inc(consts, 1)
            nc.gpsimd.memset(mhalf[:, :], -0.5).then_inc(ones_set, 1)
            nc.gpsimd.memset(zeros[:, :], 0.0).then_inc(ones_set, 1)
            nc.gpsimd.memset(epsilon[:, :], EPS).then_inc(ones_set, 1)
            nc.gpsimd.memset(lt[:, :, :, SPLIT_ROWS:LROWS], 1.0).then_inc(ones_set, 1)
            nc.gpsimd.memset(alt[:, SPLIT_ROWS:LROWS], 1.0).then_inc(ones_set, 1)
            nc.gpsimd.memset(v_all[:, :, :, HD:VW], 1.0).then_inc(ones_set, 1)
            pool.wait_ge(ones_set, 6)

            def rstd(q):
                c = slice(4 * q, 4 * q + 4)
                pool.wait_ge(mv_ready, 4 * q + 4)
                nc.gpsimd.tensor_scalar(ve[:, c], mv[:, c, 1], EPS, None, ALU.add).then_inc(ve_ready, 1)
                pool.wait_ge(ve_ready, q + 1)
                nc.gpsimd.tensor_tensor(rs[:, c], ve[:, c], mhalf[:, c], ALU.pow).then_inc(rs_ready, 1)

            rstd(0)

            def left_parts(ph, g, p, rows=bl):
                step = left_step[ph]
                shift, scale = 2 * ph * LEFT, (2 * ph + 1) * LEFT
                sh = rows[:, bass.ds(g * GB, GB), shift:shift + LEFT]
                L = lt[:, p, :, 0:SPLIT_ROWS].rearrange("p b (r w) -> p b r w", w=LEFT)
                a1 = L[:, :, 0]

                def times(v, r):
                    return v[:, :, None, :].to_broadcast([P, GB, r, LEFT])

                pool.wait_ge(xn_ready[ph], g + 1)
                nc.gpsimd.tensor_tensor(lm[:, :, :], xn[:, p, :, P:D], rows[:, bass.ds(g * GB, GB), scale:scale + LEFT],
                                        ALU.mult).then_inc(step, 1)
                pool.wait_ge(step, 4 * g + 1)
                nc.gpsimd.tensor_tensor(lv[:, :, :], lm[:, :, :], sh, ALU.add).then_inc(step, 1)
                nc.gpsimd.tensor_tensor(L[:, :, 0:3], times(lm, 3), times(sh, 3), ALU.add).then_inc(step, 1)
                pool.wait_ge(step, 4 * g + 3)
                nc.gpsimd.tensor_tensor(lr[:, :, :], lv[:, :, :], a1, ALU.subtract).then_inc(step, 1)
                nc.gpsimd.tensor_tensor(L[:, :, 3:5], times(lv, 2), times(a1, 2), ALU.subtract).then_inc(left_ready[ph], 1)
                pool.wait_ge(step, 4 * g + 4)
                pool.wait_ge(left_ready[ph], 2 * g + 1)
                nc.gpsimd.tensor_tensor(L[:, :, 5], lr[:, :, :], L[:, :, 3], ALU.subtract).then_inc(left_ready[ph], 1)

            pool.wait_ge(first_ready, 1)
            left_parts(0, 0, 0, bl_first)
            left_parts(0, 1, 1, bl_first)
            rstd(1)
            rstd(2)
            rstd(3)
            pool.wait_ge(bl_in, 16)

            def pool_phase0(g, p):
                pool.wait_ge(xt_done[0], g + 1)
                left_parts(0, g + 2, (p + 2) % RING)

            with pool.Fori(0, TURNS) as i:
                for p in range(RING):
                    pool_phase0(RING * i + p, p)

            def weight_parts2():
                c, n = slice(C_P, WCOLS), WCOLS - C_P
                steps = (
                    (wlb[:, c], wlf[:, c], zeros[0:LROWS, 0:1].to_broadcast([LROWS, n]), ALU.add),
                    (wlt[:, :], wlb[:, c], msk[:, 0:1].to_broadcast([LROWS, n]), ALU.mult),
                    (wlr[:, c], wlt[:, :], wlf[:, c], ALU.add),
                    (wlb[:, c], wlr[:, c], zeros[0:LROWS, 0:1].to_broadcast([LROWS, n]), ALU.add),
                    (wlt[:, :], wlb[:, c], msk[:, 1:2].to_broadcast([LROWS, n]), ALU.mult))
                for i, (dst, a, b, op) in enumerate(steps):
                    nc.gpsimd.tensor_tensor(dst, a, b, op).then_inc(wl2_step, 1)
                    pool.wait_ge(wl2_step, i + 1)
                nc.gpsimd.tensor_tensor(wl[:, c], wlt[:, :], wlr[:, c], ALU.add).then_inc(wl2_ready, 1)

            pool.wait_ge(wl2_in, 32)
            pool.wait_ge(wl_in, 48)
            weight_parts2()
            again(pool, WHOLE + 1, 1, TURNS, last_out)

            def alt_parts(v, n):
                pool.wait_ge(at_ready, n + 1 + SPARE)
                pool.wait_ge(att_done, 2 * n + SPARE)
                la = alt[:, 0:SPLIT_ROWS].rearrange("p (r w) -> p r w", w=LEFT)
                nc.gpsimd.tensor_tensor(la[:, 0:3], v[:, None, :].to_broadcast([P, 3, LEFT]),
                                        zeros[:, None, :].to_broadcast([P, 3, LEFT]), ALU.add).then_inc(alt_step, 1)
                pool.wait_ge(alt_step, 2 * n + 1)
                nc.gpsimd.tensor_tensor(alr[:, :], v, la[:, 0], ALU.subtract).then_inc(alt_step, 1)
                nc.gpsimd.tensor_tensor(la[:, 3:5], v[:, None, :].to_broadcast([P, 2, LEFT]),
                                        la[:, 0:1].to_broadcast([P, 2, LEFT]), ALU.subtract).then_inc(alt_ready, 1)
                pool.wait_ge(alt_step, 2 * n + 2)
                pool.wait_ge(alt_ready, 2 * n + 1)
                nc.gpsimd.tensor_tensor(la[:, 5], alr[:, :], la[:, 3], ALU.subtract).then_inc(alt_ready, 1)

            def residual(n):
                pool.wait_ge(pr_ready, n + 1 + SPARE)
                nc.gpsimd.tensor_tensor(x1[:, bass.ds(n, 1)].rearrange("p o d -> p (o d)"), pr[:, :],
                                        xs[:, bass.ds(n, 1)].rearrange("p o d -> p (o d)"), ALU.add).then_inc(x1_ready, 1)

            def rstd2(g, p):
                pool.wait_ge(mv2_ready, GB * (g + 1))
                nc.gpsimd.tensor_tensor(ve2[:, p], mv2[:, p, :, 1], epsilon[:, :], ALU.add).then_inc(ve2_ready, 1)
                pool.wait_ge(ve2_ready, g + 1)
                nc.gpsimd.tensor_tensor(rs2[:, p], ve2[:, p], mhalf[:, 0:GB], ALU.pow).then_inc(rs2_ready, 1)

            def pool_attention(u, k, it):
                if isinstance(u, int) and u == 0:
                    return
                alt_parts(at[:, P:D], u - 1)
                if isinstance(u, int) and u == B - 1:
                    left_parts(1, 0, 0)
                residual(u - 1)
                if isinstance(u, int) and u == B - 2:
                    rstd2(0, 0)
                    rstd2(1, 1)

            units(pool, pool_attention)
            alt_parts(at[:, P:D], B - 1)
            left_parts(1, 1, 1)
            residual(B - 1)

            def residual2(it, p):
                g = 2 * it + p
                for b in range(GB):
                    pool.wait_ge(fr_ready, GB * g + b + 1 + SPARE)
                    pool.wait_ge(y_out[p], 16 * it + SPARE)
                    nc.gpsimd.tensor_tensor(yo[:, p, b], fr[:, p, b],
                                            x1[:, bass.ds(g * GB + b, 1)].rearrange("p o d -> p (o d)"),
                                            ALU.add).then_inc(y_ready, 1)

            with pool.Fori(0, GROUPS // 2 - 1) as i:
                for p in range(2):
                    g = 2 * i + p
                    rstd2(g + 2, p)
                    pool.wait_ge(xt_done[1], g + 1)
                    left_parts(1, g + 2, p)
                    residual2(i, p)
            residual2(GROUPS // 2 - 1, 0)

        @block.scalar
        def _(act):
            for s in (v_copied, ex_ready, ot_copied, att_copied, g_ready):
                act.sem_inc(s, SPARE)
            act.wait_ge(cond_in, 16)
            nc.scalar.activation(ce[:, :], cs[:, :], ACT.Exp, scale=-1.0).then_inc(silu_exp, 1)

            def mod_copy(f, src):
                for q in range(2):
                    nc.scalar.activation(mod[:, 2 * f + q, :], src[:, q * B:(q + 1) * B], ACT.Copy, bias=float(q))\
                        .then_inc(mod_ready, 1)

            act.wait_ge(ada_done, 2)
            mod_copy(0, bank[2])
            act.wait_ge(spread_done, 1)
            nc.scalar.activation(bl_first[:, :, :].rearrange("p b w -> p (b w)"), bank[3][:, 0:FIRST * 2 * LEFT],
                                 ACT.Copy).then_inc(first_ready, 1)
            act.wait_ge(ada_done, 3)
            mod_copy(1, bank[5])

            def modulate(ph, g, p):
                act.wait_ge(xt_done[ph], g + 1)
                for b in range(GB):
                    s = bass.ds(g * GB + b, 1)
                    ins = nc.scalar.activation(ht[:, p, b * N:(b + 1) * N], bank[0][:, b * N:(b + 1) * N], ACT.Identity,
                                               bias=mod[:, 2 * ph, s], scale=mod[:, 2 * ph + 1, s])
                    ins.then_inc(ht_ready[ph], 1)

            act.wait_ge(mod_ready, 4)
            modulate(0, 0, 0)

            def nmt_copy(b):
                act.wait_ge(nmt_done, b + 1)
                nc.scalar.activation(nmt[:, :], bank[6][0:PARTS * H, 2 * N:2 * N + N // 2].bitcast(BF16), ACT.Copy)\
                    .then_inc(nmt_copied, 1)

            def act_phase0(it, p, last):
                g = RING * it + p
                act.wait_ge(parts_out[p], 16 * GB * it + SPARE)
                for c in range(QKC):
                    if c == 2 and not last:
                        modulate(0, g + 1, (p + 1) % RING)
                    if scored(g) == 1 and c == 1:
                        nmt_copy(0)
                    act.wait_ge(qk_done, QKC * g + c + 1)
                    nc.scalar.activation(qkp[:, p, 0, c, :], bank[2 + c][0:QKR, 0:GT], ACT.Copy).then_inc(hi_ready, 1)
                act.wait_ge(v_done, g + 1)
                nc.scalar.activation(v_all[:, bass.ds(g * GB, GB), :, 0:HD].rearrange("p b h d -> p (b h) d"),
                                     bank[5][:, 0:GB * D].rearrange("p (k d) -> p k d", d=HD),
                                     ACT.Copy).then_inc(v_copied, 1)
                for c in range(QKC):
                    act.wait_ge(rest_ready, QKC * g + c + 1 + SPARE)
                    nc.scalar.activation(qkp[:, p, 1, c, :], qkr[:, p, c, :], ACT.Copy).then_inc(mid_ready, 1)

            with act.Fori(0, TURNS) as i:
                for p in range(RING):
                    act_phase0(i, p, False)
            act_phase0(TURNS, 0, False)
            act_phase0(TURNS, 1, True)

            def att_copy(n):
                act.wait_ge(att_done, 2 * n + 1 + SPARE)
                act.wait_ge(proj_done, n + SPARE)
                nc.scalar.activation(att[:, :], bank[6][:, 0:N], ACT.Copy).then_inc(att_copied, 1)
                act.wait_ge(att_done, 2 * (n + 1) + SPARE)
                nc.scalar.activation(atl[:, :], bank[7][0:LROWS, 2 * N:2 * N + N // 2].bitcast(BF16), ACT.Copy)\
                    .then_inc(att_copied, 1)

            def act_attention(u, k, it):
                for i in range(QUADS):
                    act.wait_ge(st_done, QUADS * u + i + 1 + SPARE)
                    act.wait_ge(pv_done, QUADS * (u - 1) + i + 1 + SPARE)
                    nc.scalar.activation(ex[:, i, :], bank[2 + i % 2][:, :], ACT.Exp, scale=SCALE).then_inc(ex_ready, 1)
                    if i == 1 and ahead(u, 1):
                        act.wait_ge(max_in, 16 * (u + 1))
                        nmt_copy(u + 1)
                if not (isinstance(u, int) and u == 0):
                    att_copy(u - 1)
                act.wait_ge(pv_done, QUADS * (u + 1) + SPARE)
                act.wait_ge(on_done, u + SPARE)
                nc.scalar.activation(ot[:, :], bank[4][:, :], ACT.Copy).then_inc(ot_copied, 1)

            units(act, act_attention)

            modulate(1, 0, 0)
            att_copy(B - 1)

            def act_mlp(g, p, last):
                for c, (_, m) in enumerate(HCH):
                    act.wait_ge(f1_done, NCH * g + c + 1)
                    act.wait_ge(f2_done, GB * (g - 1) + SPARE)
                    nc.scalar.activation(hg[0:m, p, c, :], bank[2 + c % 4][0:m, 0:GT], ACT.Gelu_apprx_tanh)\
                        .then_inc(g_ready, 1)
                    if c == 2 and not last:
                        modulate(1, g + 1, 1 - p)

            act_mlp(0, 0, False)
            with act.Fori(0, GROUPS // 2 - 1) as i:
                for p in range(2):
                    act_mlp(2 * i + 1 + p, 1 - p, False)
            act_mlp(GROUPS - 1, 1, True)

        @block.vector
        def _(dve):
            for s in (lo_ready, rest_ready, pr_ready, at_ready, fr_ready):
                dve.sem_inc(s, SPARE)
            nc.vector.memset(bank[4][:, :], 0.0).then_inc(set_by_dve, 1)
            nc.vector.memset(ctl[:, :], 1.0).then_inc(silu_step, 1)
            nc.vector.memset(ones[:, :], 1.0).then_inc(set_by_dve, 1)
            nc.vector.memset(hg[96:97, :, NCH - 1, :], 1.0).then_inc(set_by_dve, 1)
            dve.wait_ge(silu_exp, 1)
            nc.vector.tensor_scalar(cr[:, :], ce[:, :], 1.0, None, ALU.add).then_inc(silu_step, 1)
            dve.wait_ge(silu_step, 2)
            nc.vector.reciprocal(ce[:, :], cr[:, :]).then_inc(silu_step, 1)
            dve.wait_ge(silu_step, 3)
            nc.vector.tensor_tensor(cr[:, :], cs[:, :], ce[:, :], ALU.mult).then_inc(silu_ready, 1)
            dve.wait_ge(ct_turned, 1)
            nc.vector.tensor_copy(ct[:, :], bank[0][:, 0:B]).then_inc(ct_copied, 1)
            nc.vector.tensor_copy(ctl[0:LEFT, :], bank[0][0:LEFT, B:2 * B]).then_inc(ct_copied, 1)

            def statistics(q):
                dve.wait_ge(x_in[q], 16)
                for b in range(4 * q, 4 * q + 4):
                    nc.vector.bn_stats(st[:, b, :], xs[:, b, :]).then_inc(stat_step, 1)
                for b in range(4 * q, 4 * q + 4):
                    dve.wait_ge(stat_step, b + 1)
                    nc.vector.bn_aggr(mv[:, b, :], st[:, b, :]).then_inc(mv_ready, 1)

            statistics(0)
            dve.wait_ge(ada_done, 1)
            rows = bank[6][0:B, 0:6 * LEFT].rearrange("b (f q w) -> b f q w", f=2, w=LEFT)
            left_rows = left_r[:, :].rearrange("b (f q w) -> b f q w", f=2, w=LEFT)
            nc.vector.tensor_copy(left_rows[:, :, 0], rows[:, :, 0]).then_inc(rows_ready, 1)
            nc.vector.tensor_scalar(left_rows[:, :, 1], rows[:, :, 1], 1.0, None, ALU.add).then_inc(rows_ready, 1)
            dve.wait_ge(rows_ready, 2)
            dve.wait_ge(consts, 2)
            nc.vector.tensor_tensor(spread[:, :, :], left_r[:, None, 0:2 * LEFT].to_broadcast([B, FIRST, 2 * LEFT]),
                                    ident[0:B, 0:FIRST, None].to_broadcast([B, FIRST, 2 * LEFT]),
                                    ALU.mult).then_inc(spread_ready, 1)

            def weight_parts(i):
                c = slice(0, C_P)
                if i > 0:
                    dve.wait_ge(wl_step, 2 * i)
                nc.vector.tensor_copy(wlb[:, c], (wlf, wlr)[i][:, c]).then_inc(wl_step, 1)
                dve.wait_ge(wl_step, 2 * i + 1)
                nc.vector.scalar_tensor_tensor(out=(wlr, wl)[i][:, c], in0=wlb[:, c], scalar=msk[:, i:i + 1],
                                               in1=(wlf, wlr)[i][:, c], op0=ALU.mult, op1=ALU.add)\
                    .then_inc((wl_step, wl_ready)[i], 1)

            def normalise(ph, g, p):
                for b in range(GB):
                    s = bass.ds(g * GB + b, 1)
                    src = (xs, x1)[ph][:, s].rearrange("p o d -> p (o d)")
                    mean = mv[:, s, 0] if ph == 0 else mv2[:, p, b, 0:1]
                    rstd = rs[:, s] if ph == 0 else rs2[:, p, b:b + 1]
                    ins = nc.vector.tensor_scalar(xn[:, p, b, :], src, mean, rstd, ALU.subtract, ALU.mult)
                ins.then_inc(xn_ready[ph], 1)

            def left_copy(ph, g, p):
                dve.wait_ge(xt_done[ph], g + 1)
                nc.vector.tensor_copy(hl[:, p, :], bank[1][0:LROWS, 0:GT // 2].bitcast(BF16)).then_inc(hl_ready[ph], 1)

            dve.wait_ge(wl_in, 48)
            weight_parts(0)
            dve.wait_ge(rs_ready, 1)
            normalise(0, 0, 0)
            weight_parts(1)
            normalise(0, 1, 1)
            statistics(1)
            left_copy(0, 0, 0)
            dve.wait_ge(ada_done, 4)
            nc.vector.tensor_copy(gate_r[:, :], bank[7][0:B, 0:2 * D]).then_inc(rows_ready, 1)
            statistics(2)
            statistics(3)
            dve.wait_ge(rs_ready, 2)

            def negated_max(b, q, i):
                dve.wait_ge(s_done, QUADS * b + i + 1)
                nc.vector.tensor_reduce(nm[:, q, 4 * i:4 * i + 4], score_bank(b, i)[:, :].rearrange("p (h m) -> p h m", h=4),
                                        AX.X, ALU.max, negate=True).then_inc(max_ready, 1)

            def max_parts(b, q):
                dve.wait_ge(max_ready, QUADS * (b + 1))
                dve.wait_ge(nmt_done, b)
                nc.vector.tensor_copy(nmp[:, 0, :], nm[:, q, :]).then_inc(nm_step, 1)
                dve.wait_ge(nm_step, 3 * b + 1)
                nc.vector.tensor_tensor(nmr[:, :], nm[:, q, :], nmp[:, 0, :], ALU.subtract).then_inc(nm_step, 1)
                nc.vector.tensor_tensor(nmp[:, 1, :], nm[:, q, :], nmp[:, 0, :], ALU.subtract).then_inc(nm_step, 1)
                dve.wait_ge(nm_step, 3 * b + 3)
                nc.vector.tensor_tensor(nmp[:, 2, :], nmr[:, :], nmp[:, 1, :], ALU.subtract).then_inc(nm_ready, 1)

            def dve_phase0(g, p, more, last):
                if more:
                    if p == 2:
                        dve.wait_ge(rs_ready, 4)
                    dve.wait_ge(xt_done[0], g + 1)
                    normalise(0, g + 2, (p + 2) % RING)
                dve.wait_ge(lo_ready, QKC * (g - 1) + SPARE)
                for c in range(QKC):
                    if c == 1 and not last:
                        left_copy(0, g + 1, (p + 1) % RING)
                    dve.wait_ge(hi_ready, QKC * g + c + 1)
                    nc.vector.tensor_tensor(qkr[:, p, c, :], bank[2 + c][0:QKR, 0:GT], qkp[:, p, 0, c, :],
                                            ALU.subtract).then_inc(rest_ready, 1)
                    if scored(g) is not None and c < 2:
                        negated_max(scored(g), scored(g), c)
                if scored(g) is not None:
                    negated_max(scored(g), scored(g), 2)
                    negated_max(scored(g), scored(g), 3)
                    max_parts(scored(g), scored(g))
                for c in range(QKC):
                    dve.wait_ge(mid_ready, QKC * g + c + 1)
                    nc.vector.tensor_tensor(qkp[:, p, 2, c, :], qkr[:, p, c, :], qkp[:, p, 1, c, :],
                                            ALU.subtract).then_inc(lo_ready, 1)

            with dve.Fori(0, TURNS) as i:
                for p in range(RING):
                    dve_phase0(RING * i + p, p, True, False)
            dve_phase0(WHOLE, 0, False, False)
            dve_phase0(WHOLE + 1, 1, False, True)

            heads = bank[5][:, :].rearrange("p (h w) -> p h w", h=H)

            def dve_denominators(n):
                dve.wait_ge(on_done, n + 1 + SPARE)
                nc.vector.reciprocal(rd[:, :], heads[:, :, HD]).then_inc(rd_ready, 1)

            def dve_divide(n):
                dve.wait_ge(rd_ready, n + 1)
                dve.wait_ge(att_done, 2 * n + SPARE)
                nc.vector.tensor_tensor(at[:, :].rearrange("p (h d) -> p h d", h=H), heads[:, :, 0:HD],
                                        rd[:, :, None].to_broadcast([P, H, HD]), ALU.mult).then_inc(at_ready, 1)

            def gate(n):
                dve.wait_ge(proj_done, n + 1 + SPARE)
                dve.wait_ge(x1_ready, n + SPARE)
                nc.vector.tensor_tensor(pr[:, :], bank[7][:, 0:D], gates[:, bass.ds(n, 1), 0:D].rearrange("p o d -> p (o d)"),
                                        ALU.mult).then_inc(pr_ready, 1)

            dve.wait_ge(gates_in[0], 16)

            def statistics2(g, p):
                for b in range(GB):
                    dve.wait_ge(x1_ready, GB * g + b + 1 + SPARE)
                    nc.vector.bn_stats(st2[:, p, b, :], x1[:, bass.ds(g * GB + b, 1)].rearrange("p o d -> p (o d)"))\
                        .then_inc(st2_done, 1)
                dve.wait_ge(st2_done, GB * (g + 1))
                dve.sem_inc(passed, 1)
                for b in range(GB):
                    nc.vector.bn_aggr(mv2[:, p, b, :], st2[:, p, b, :]).then_inc(mv2_ready, 1)

            def dve_attention(u, k, it):
                tail = not (isinstance(u, int) and u == 0)
                if tail:
                    dve_denominators(u - 1)
                    dve_divide(u - 1)
                if ahead(u, 2):
                    for i in range(QUADS):
                        negated_max(u + 2, k % 2, i)
                    max_parts(u + 2, k % 2)
                if isinstance(u, int) and u == B - 1:
                    for g in range(2):
                        dve.wait_ge(rs2_ready, g + 1)
                        normalise(1, g, g)
                if tail:
                    gate(u - 1)
                if isinstance(u, int) and u == B - 2:
                    statistics2(0, 0)
                    statistics2(1, 1)

            units(dve, dve_attention)
            dve_denominators(B - 1)
            dve_divide(B - 1)
            left_copy(1, 0, 0)

            dve.wait_ge(gates_in[1], 16)

            def gate2(g, p, last=False):
                for b in range(GB):
                    dve.wait_ge(f2_done, GB * g + b + 1 + SPARE)
                    dve.wait_ge(y_ready, GB * (g - 1) + SPARE)
                    nc.vector.tensor_tensor(fr[:, p, b, :], bank[6 + b][:, 0:D],
                                            gates[:, bass.ds(g * GB + b, 1), D:2 * D].rearrange("p o d -> p (o d)"),
                                            ALU.mult).then_inc(fr_ready, 1)
                    if last:
                        dve.wait_ge(fr_ready, GB * g + b + 1 + SPARE)
                        dve.wait_ge(y_out[p], SPARE + 16 * (GROUPS // 2 - 1))
                        nc.vector.tensor_tensor(yo[:, p, b], fr[:, p, b], x1[:, g * GB + b, :],
                                                ALU.add).then_inc(last_ready, 1)

            def dve_mlp(g, p, more):
                first = isinstance(g, int) and g == 0
                if first:
                    gate(B - 1)
                    left_copy(1, 1, 1)
                if more:
                    statistics2(g + 2, p)
                    dve.wait_ge(rs2_ready, g + 3)
                    dve.wait_ge(xt_done[1], g + 1)
                    normalise(1, g + 2, p)
                if not first:
                    left_copy(1, g + 1, 1 - p)
                gate2(g, p)

            dve_mlp(0, 0, True)
            with dve.Fori(0, GROUPS // 2 - 2) as i:
                for p in range(2):
                    dve_mlp(2 * i + 1 + p, 1 - p, True)
            dve_mlp(GROUPS - 3, 1, True)
            dve_mlp(GROUPS - 2, 0, False)
            gate2(GROUPS - 1, 1, True)

        @block.tensor
        def _(pe):
            for s in (pv_done, st_done, on_done, att_done, proj_done, f2_done):
                pe.sem_inc(s, SPARE)
            pe.wait_ge(consts, 2)
            pe.wait_ge(silu_ready, 1)
            nc.tensor.transpose(bank[0][:, 0:B], cr[:, 0:P], ident[0:B, 0:B])
            nc.tensor.transpose(bank[0][0:LEFT, B:2 * B], cr[:, P:D], ident[0:B, 0:B]).then_inc(ct_turned, 1)
            pe.wait_ge(ct_copied, 2)
            pe.wait_ge(wa_in, 32)
            last_dims = (wa[:, :].rearrange("p (q d) -> p q d", d=D), wal[:, :].rearrange("p (q d) -> p q d", d=D))
            nc.tensor.matmul(bank[6][0:B, 0:6 * LEFT], ct[:, :], last_dims[0][:, :, P:D], start=True, stop=False)
            nc.tensor.matmul(bank[6][0:B, 0:6 * LEFT], ctl[:, :], last_dims[1][:, :, P:D], start=False, stop=True)\
                .then_inc(ada_done, 1)

            def mod_products(f, dst):
                for n in range(2):
                    c = slice((3 * f + n) * D, (3 * f + n) * D + P)
                    nc.tensor.matmul(dst[:, n * B:(n + 1) * B], wa[:, c], ct[:, :], start=True, stop=False)
                    mm = nc.tensor.matmul(dst[:, n * B:(n + 1) * B], wal[:, c], ctl[:, :], start=False, stop=True)
                mm.then_inc(ada_done, 1)

            mod_products(0, bank[2])
            pe.wait_ge(spread_ready, 1)
            pe.wait_ge(set_by_dve, 3)
            nc.tensor.matmul(bank[3][:, 0:FIRST * 2 * LEFT], ones[:, :], spread[:, :, :].rearrange("b f w -> b (f w)"),
                             start=True, stop=True).then_inc(spread_done, 1)
            mod_products(1, bank[5])

            def turn(ph, g, p):
                pe.wait_ge(xn_ready[ph], g + 1)
                for b in range(GB):
                    nc.tensor.transpose(bank[0][:, b * N:(b + 1) * N], xn[:, p, b, 0:P], ident[:, :])
                pe.wait_ge(left_ready[ph], 2 * (g + 1))
                parts = bank[1][0:LROWS, 0:GT // 2].bitcast(BF16)
                for b in range(GB):
                    mm = nc.tensor.transpose(parts[:, b * N:(b + 1) * N], lt[:, p, b, :], ident_b[:, :])
                mm.then_inc(xt_done[ph], 1)

            pe.wait_ge(ones_set, 6)
            turn(0, 0, 0)
            nc.tensor.matmul(bank[7][0:B, 0:2 * D], ct[:, :], last_dims[0][:, 2:6:3, :], start=True, stop=False)
            nc.tensor.matmul(bank[7][0:B, 0:2 * D], ctl[:, :], last_dims[1][:, 2:6:3, :], start=False, stop=True)\
                .then_inc(ada_done, 1)
            pe.wait_ge(wm_in, 16)
            pe.wait_ge(wl_ready, 1)
            pe.wait_ge(mod_ready, 4)
            pe.wait_ge(first_ready, 1)

            def scores_q(b, slot, i):
                for j in range(4):
                    mm = nc.tensor.matmul(score_bank(b, i)[:, j * N:(j + 1) * N], qt[0:MAX_ROW, slot, head(i, j)],
                                          kt[0:MAX_ROW, slot, head(i, j)], start=True, stop=True)
                mm.then_inc(s_done, 1)

            def turn_max():
                pe.sem_inc(passed, 1)
                nc.tensor.transpose(bank[6][0:PARTS * H, 2 * N:2 * N + N // 2].bitcast(BF16),
                                    nmp[:, :, :].rearrange("p l h -> p (l h)"), ident_b[:, :]).then_inc(nmt_done, 1)

            def pe_phase0(g, p, last):
                pe.wait_ge(ht_ready[0], GB * (g + 1))
                pe.wait_ge(hl_ready[0], g + 1)
                for c in range(QKC):
                    if c == 2 and not last:
                        turn(0, g + 1, (p + 1) % RING)
                    pe.wait_ge(rest_ready, QKC * (g - 1) + c + 1 + SPARE)
                    w = slice(c * QKR, (c + 1) * QKR)
                    dst = bank[2 + c][0:QKR, 0:GT]
                    nc.tensor.matmul(dst, wm[:, w], ht[:, p, :], start=True, stop=False)
                    nc.tensor.matmul(dst, wl[:, w], hl[:, p, :], start=False, stop=True).then_inc(qk_done, 1)
                    if scored(g) is not None and c < 2:
                        b = scored(g)
                        pe.wait_ge(qk_in[b], 32)
                        if b == 0 and c == 0:
                            pe.wait_ge(fill_in, 32)
                            pe.wait_ge(rows_ready, 3)
                        scores_q(b, b, c)
                        if b == 1 and c == 0:
                            pe.wait_ge(nm_ready, 1)
                            turn_max()
                pe.wait_ge(v_copied, g + SPARE)
                for b in range(GB):
                    dst, t = bank[5][:, b * D:(b + 1) * D], slice(b * N, (b + 1) * N)
                    nc.tensor.matmul(dst, ht[:, p, t], wm[:, C_V:C_P], start=True, stop=False)
                    mm = nc.tensor.matmul(dst, hl[:, p, t], wl[:, C_V:C_P], start=False, stop=True)
                mm.then_inc(v_done, 1)
                if scored(g) is not None:
                    for i in range(2, QUADS):
                        pe.wait_ge(max_ready, QUADS * scored(g) + i - 1)
                        scores_q(scored(g), scored(g), i)

            with pe.Fori(0, TURNS) as i:
                for p in range(RING):
                    pe_phase0(RING * i + p, p, False)
            pe_phase0(WHOLE, 0, False)
            pe_phase0(WHOLE + 1, 1, True)

            def scores_k(slot, i):
                for j in range(4):
                    mm = nc.tensor.matmul(bank[2 + i % 2][:, j * N:(j + 1) * N], kt[0:SROWS, slot, head(i, j)],
                                          qt[0:SROWS, slot, head(i, j)], start=True, stop=True)
                mm.then_inc(st_done, 1)

            def values(slot, i):
                for j in range(4):
                    mm = nc.tensor.matmul(bank[4][32 * j:32 * j + VW, i * N:(i + 1) * N], vt[:, slot, 4 * i + j, :],
                                          ex[:, i, j * N:(j + 1) * N], start=True, stop=True)
                mm.then_inc(pv_done, 1)

            pe.wait_ge(set_by_dve, 3)
            pe.wait_ge(rest_ready, QKC * GROUPS + SPARE)
            pe.wait_ge(v_copied, GROUPS + SPARE)

            def turn_result(n):
                pe.wait_ge(ot_copied, n + 1 + SPARE)
                pe.wait_ge(at_ready, n + SPARE)
                for i in range(QUADS):
                    mm = nc.tensor.transpose(bank[5][:, i * N:(i + 1) * N], ot[:, i * N:(i + 1) * N], ident[:, :])
                mm.then_inc(on_done, 1)

            def turn_back(n):
                pe.wait_ge(at_ready, n + 1 + SPARE)
                nc.tensor.transpose(bank[6][:, 0:N], at[:, 0:P], ident[:, :]).then_inc(att_done, 1)

            def turn_back_parts(n):
                pe.wait_ge(alt_ready, 2 * (n + 1))
                pe.wait_ge(pr_ready, n + SPARE)
                nc.tensor.transpose(bank[7][0:LROWS, 2 * N:2 * N + N // 2].bitcast(BF16), alt[:, :], ident_b[:, :])\
                    .then_inc(att_done, 1)

            def project(n):
                pe.wait_ge(att_copied, 2 * (n + 1) + SPARE)
                nc.tensor.matmul(bank[7][:, 0:D], att[:, :], wm[:, C_P:C_F], start=True, stop=False)
                nc.tensor.matmul(bank[7][:, 0:D], atl[:, :], wl[:, C_P:C_F], start=False, stop=True).then_inc(proj_done, 1)

            def pe_attention(u, k, it):
                tail = not (isinstance(u, int) and u == 0)
                k2 = (k + 2) % SLOTS

                def keys(i):
                    pe.wait_ge(ex_ready, QUADS * u + i - 1 + SPARE)
                    scores_k(k % SLOTS, i)

                def pv(i):
                    pe.wait_ge(ex_ready, QUADS * u + i + 1 + SPARE)
                    values(k % SLOTS, i)

                def queries(i):
                    if ahead(u, 2):
                        pe.wait_ge(max_ready, QUADS * (u + 2) + i - 1)
                        scores_q(u + 2, k2, i)

                pe.wait_ge(max_in, 16 * (u + 1))
                keys(0)
                keys(1)
                if tail:
                    turn_result(u - 1)
                if ahead(u, 1):
                    pe.wait_ge(nm_ready, u + 2)
                    pe.wait_ge(att_copied, 2 * (u - 1) + SPARE)
                    turn_max()
                if ahead(u, 2):
                    pe.wait_ge(qk_in[k2], 32 * (it + 1 + (k + 2) // SLOTS))
                queries(0)
                pe.wait_ge(v_in[k % SLOTS], 16 * (it + 1 + k // SLOTS))
                pe.wait_ge(ot_copied, u + SPARE)
                pv(0)
                keys(2)
                queries(1)
                pv(1)
                keys(3)
                if tail:
                    if ahead(u, 1):
                        pe.wait_ge(nmt_copied, u + 2)
                    turn_back(u - 1)
                queries(2)
                pv(2)
                if tail:
                    turn_back_parts(u - 1)
                queries(3)
                pv(3)
                if tail:
                    project(u - 1)
                else:
                    pe.wait_ge(wl2_ready, 1)

            pe.wait_ge(wrest_in, 16)
            units(pe, pe_attention)

            turn_result(B - 1)
            turn(1, 0, 0)
            pe.wait_ge(w2_in, 48)
            pe.wait_ge(ex_ready, QUADS * B + SPARE)

            def pe_mlp(g, p, last):
                def hidden(c):
                    before = NCH * g if c == 0 else NCH * g + 1 if c == 4 else NCH * (g - 1) + c + 1
                    pe.wait_ge(g_ready, before + SPARE)
                    h0, m = HCH[c]
                    w = slice(C_F + h0, C_F + h0 + m)
                    dst = bank[2 + c % 4][0:m, 0:GT]
                    nc.tensor.matmul(dst, wm[:, w], ht[:, p, :], start=True, stop=False)
                    nc.tensor.matmul(dst, wl[:, w], hl[:, p, :], start=False, stop=True).then_inc(f1_done, 1)

                first = isinstance(g, int) and g == 0
                pe.wait_ge(ht_ready[1], GB * (g + 1))
                pe.wait_ge(hl_ready[1], g + 1)
                hidden(0)
                if first:
                    turn_back(B - 1)
                    turn_back_parts(B - 1)
                hidden(1)
                if first:
                    project(B - 1)
                hidden(2)
                if not last:
                    turn(1, g + 1, 1 - p)
                hidden(3)
                hidden(4)
                for b in range(GB):
                    if first and b == 1:
                        pe.wait_ge(pr_ready, B + SPARE)
                    pe.wait_ge(fr_ready, GB * (g - 1) + b + 1 + SPARE)
                    for c, (_, m) in enumerate(HCH):
                        rows = m + (c == NCH - 1)
                        if b == 0:
                            pe.wait_ge(g_ready, NCH * g + c + 1 + SPARE)
                        mm = nc.tensor.matmul(bank[6 + b][:, 0:D], hg[0:rows, p, c, b * N:(b + 1) * N],
                                              w2[0:rows, c, :], start=(c == 0), stop=(c == NCH - 1))
                    mm.then_inc(f2_done, 1)

            pe_mlp(0, 0, False)
            with pe.Fori(0, GROUPS // 2 - 1) as i:
                for p in range(2):
                    pe_mlp(2 * i + 1 + p, 1 - p, False)
            pe_mlp(GROUPS - 1, 1, True)


def part_masks():
    part = np.array([n for m in range(PARTS) for n in range(PARTS - m) for _ in range(LEFT)] + list(range(PARTS)))
    return np.stack([-(part > 0).astype(np.float32), -(part > 1).astype(np.float32)], axis=1)


def below_products():
    rows = np.zeros((SROWS - PROD_ROWS, H * N // 2), np.float32)
    rows[MAX_ROW - PROD_ROWS:] = BF16_ONES
    return rows


def kernel(x, cond_1152, L0_cond_w_qkv, L0_cond_b_qkv, L0_cond_w_proj, L0_cond_b_proj, L0_cond_w_fc1,
           L0_cond_b_fc1, L0_cond_w_fc2, L0_cond_b_fc2, L0_cond_w_ada, L0_cond_b_ada):
    from concourse import bacc
    from concourse.bass_utils import run_bass_kernel_spmd

    def with_bias(w, b):
        return np.concatenate([np.asarray(w), np.asarray(b)[None]], axis=0)

    qkv = with_bias(L0_cond_w_qkv, L0_cond_b_qkv)
    qk = qkv[:, 0:2 * D].reshape(D + 1, 2, H, QKC, HD // QKC).transpose(0, 3, 4, 1, 2).reshape(D + 1, 2 * D)
    arrays = {
        "x": np.asarray(x),
        "cond": np.asarray(cond_1152),
        "w_all": np.concatenate([qk, qkv[:, 2 * D:], with_bias(L0_cond_w_proj, L0_cond_b_proj),
                                 with_bias(L0_cond_w_fc1, L0_cond_b_fc1)], axis=1),
        "w_fc2": with_bias(L0_cond_w_fc2, L0_cond_b_fc2),
        "w_ada": with_bias(L0_cond_w_ada, L0_cond_b_ada),
        "masks": part_masks(),
        "fill": below_products(),
    }
    arrays = {f"in_{k}": np.ascontiguousarray(a) for k, a in arrays.items()}
    nc = bacc.Bacc("TRN2", target_bir_lowering=False, num_devices=1)
    args = [nc.dram_tensor(k, a.shape, mybir.dt.from_np(a.dtype), kind="ExternalInput").ap() for k, a in arrays.items()]
    args.append(nc.dram_tensor("out_x", (B, N, D), F32, kind="ExternalOutput").ap())
    build(nc, *args)
    result = run_bass_kernel_spmd(nc, [arrays], core_ids=[0])
    return result.results[0]["out_x"]
```
